# Optimizing a Trainium2 kernel written in Bass

```python
import numpy as np
import jax
import jax.numpy as jnp

def _softmax(x, axis=-1):
    return jax.nn.softmax(x, axis=axis)

def _gelu(x):
    return jax.nn.gelu(x, approximate=True)

def _silu(x):
    return jax.nn.silu(x)

def _sigmoid(x):
    return jax.nn.sigmoid(x)

def _layernorm(x, axis=-1, eps=1e-05):
    m = jnp.mean(x, axis=axis, keepdims=True)
    v = jnp.var(x, axis=axis, keepdims=True)
    return (x - m) / jnp.sqrt(v + eps)

def _scatter_add(tgt, idx, src, axis=0):
    return tgt.at[idx].add(src)

def _segment_sum(src, seg, n):
    return jax.ops.segment_sum(src, seg, n)
kernel_name = 'mk_recurrent_d1_jaxref_r8_073b31'

def setup_inputs(seed: int=0):
    np.random.seed(seed)
    _w = jnp.asarray

    def _L0_attn_setup():
        import jax, jax.numpy as jnp
        import numpy as np
        D_MODEL = 256
        NHEAD = 16
        LN_EPS = 1e-05
        key = jax.random.key(seed)
        ks = jax.random.split(key, 6)
        scale = 1.0 / np.sqrt(D_MODEL)
        return {'x': jax.random.normal(ks[0], (4, 512, D_MODEL), dtype=jnp.float32), 'Wq': jax.random.normal(ks[1], (D_MODEL, D_MODEL), dtype=jnp.float32) * scale, 'Wv': jax.random.normal(ks[2], (D_MODEL, D_MODEL), dtype=jnp.float32) * scale, 'Wg': jax.random.normal(ks[3], (D_MODEL, D_MODEL), dtype=jnp.float32) * scale, 'Wo': jax.random.normal(ks[4], (D_MODEL, D_MODEL), dtype=jnp.float32) * scale, 'beta': jnp.full((NHEAD,), -0.2, dtype=jnp.float32), 'ln_g': jnp.ones((D_MODEL,), dtype=jnp.float32), 'ln_b': jnp.zeros((D_MODEL,), dtype=jnp.float32)}
    _L0_attn_in = _L0_attn_setup()

    def _L0_ffn_setup():
        import jax, jax.numpy as jnp
        import numpy as np
        NUM_EXPERTS = 8
        TOP_K = 2
        key = jax.random.key(seed)
        ks = jax.random.split(key, 5)
        B, L, D, H = (2, 256, 256, 512)
        return {'layer_input': jax.random.normal(ks[0], (B, L, D), jnp.float32), 'router_weight': jax.random.normal(ks[1], (NUM_EXPERTS, D), jnp.float32) * 0.02, 'w_in': jax.random.normal(ks[2], (NUM_EXPERTS, 2 * H, D), jnp.float32) * 0.02, 'w_out': jax.random.normal(ks[3], (NUM_EXPERTS, D, H), jnp.float32) * 0.02, 'bias': jax.random.normal(ks[4], (D,), jnp.float32) * 0.02}
    _L0_ffn_in = _L0_ffn_setup()
    _d = {'L0_attn_x': _L0_attn_in['x'], 'L0_attn_Wq': _L0_attn_in['Wq'], 'L0_attn_Wv': _L0_attn_in['Wv'], 'L0_attn_Wg': _L0_attn_in['Wg'], 'L0_attn_Wo': _L0_attn_in['Wo'], 'L0_attn_beta': _L0_attn_in['beta'], 'L0_attn_ln_g': _L0_attn_in['ln_g'], 'L0_attn_ln_b': _L0_attn_in['ln_b'], 'L0_ffn_router_weight': _L0_ffn_in['router_weight'], 'L0_ffn_w_in': _L0_ffn_in['w_in'], 'L0_ffn_w_out': _L0_ffn_in['w_out'], 'L0_ffn_bias': _L0_ffn_in['bias']}
    _x0 = _d['L0_attn_x']
    _d['L0_attn_x'] = jax.random.normal(jax.random.fold_in(jax.random.key(seed), 1), (8, 512, 256), dtype=_x0.dtype)
    del _x0
    return _d

def reference(L0_attn_x, L0_attn_Wq, L0_attn_Wv, L0_attn_Wg, L0_attn_Wo, L0_attn_beta, L0_attn_ln_g, L0_attn_ln_b, L0_ffn_router_weight, L0_ffn_w_in, L0_ffn_w_out, L0_ffn_bias):

    def _L0_attn_ref(x, Wq, Wv, Wg, Wo, beta, ln_g, ln_b):
        import jax, jax.numpy as jnp
        import numpy as np
        D_MODEL = 256
        NHEAD = 16
        LN_EPS = 1e-05
        B, S, D = x.shape
        H = NHEAD
        Dh = D // H
        q = (x @ Wq).reshape(B, S, H, Dh)
        v = (x @ Wv).reshape(B, S, H, Dh)
        lam = jax.nn.sigmoid(beta)[None, :, None]
        v_t = jnp.moveaxis(v, 1, 0)

        def step(prev, vt):
            new = lam * prev + vt
            return (new, new)
        _, rest = jax.lax.scan(step, v_t[0], v_t[1:])
        states = jnp.concatenate([v_t[:1], rest], axis=0)
        states = jnp.moveaxis(states, 0, 1)
        y = (q * states).reshape(B, S, D)
        mu = jnp.mean(y, axis=-1, keepdims=True)
        var = jnp.var(y, axis=-1, keepdims=True)
        y = (y - mu) * jax.lax.rsqrt(var + LN_EPS) * ln_g + ln_b
        gate = jax.nn.silu(x @ Wg)
        y = y * gate
        return y @ Wo

    def _L0_ffn_ref(layer_input, router_weight, w_in, w_out, bias):
        import jax, jax.numpy as jnp
        import numpy as np
        NUM_EXPERTS = 8
        TOP_K = 2
        B, L, D = layer_input.shape
        x = layer_input.reshape(-1, D)
        T = x.shape[0]
        logits = (x @ router_weight.T).astype(jnp.float32)
        top_vals, top_idx = jax.lax.top_k(logits, TOP_K)
        top_gates = jax.nn.softmax(top_vals, axis=1).astype(x.dtype)
        dense_gates = jnp.zeros((T, NUM_EXPERTS), x.dtype)
        dense_gates = dense_gates.at[jnp.arange(T)[:, None], top_idx].set(top_gates)

        def expert_step(acc, ew):
            wi, wo, g = ew
            h = x @ wi.T
            a, b = jnp.split(h, 2, axis=-1)
            o = jax.nn.silu(a) * b @ wo.T
            return (acc + g[:, None] * o, None)
        acc, _ = jax.lax.scan(expert_step, jnp.zeros_like(x), (w_in, w_out, dense_gates.T))
        return acc.reshape(B, L, D) + bias
    x = L0_attn_x
    xn = _layernorm(x, axis=-1)
    s = _L0_attn_ref(xn, L0_attn_Wq, L0_attn_Wv, L0_attn_Wg, L0_attn_Wo, L0_attn_beta, L0_attn_ln_g, L0_attn_ln_b)
    g = _silu(_L0_ffn_ref(xn, L0_ffn_router_weight, L0_ffn_w_in, L0_ffn_w_out, L0_ffn_bias))
    x = x + s * g
    return x

_drawn_inputs = setup_inputs


def setup_inputs(seed=0):
    import zlib

    import numpy as np

    out = dict(_drawn_inputs(seed))
    spreads = {'L0_attn_beta': (-0.20000000298023224, 0.6),
     'L0_attn_ln_g': (1.0, 0.6),
     'L0_attn_ln_b': (0.0, 0.8)}
    factors = {'L0_attn_Wq': 6.976,
     'L0_attn_Wv': 6.883,
     'L0_attn_Wg': 7.312,
     'L0_attn_Wo': 6.877,
     'L0_ffn_router_weight': 8.0,
     'L0_ffn_w_in': 8.0,
     'L0_ffn_w_out': 8.0,
     'L0_ffn_bias': 37.82}
    for name, (base, spread) in spreads.items():
        noise = np.random.default_rng([zlib.crc32(name.encode()), seed]).standard_normal(out[name].shape)
        drawn = base * np.exp(spread * noise) if base else spread * noise
        out[name] = jnp.asarray(drawn.astype(out[name].dtype))
    for name, factor in factors.items():
        out[name] = (out[name] * factor).astype(out[name].dtype)
    return out
```

```python
from contextlib import ExitStack

import numpy as np

import concourse.bass as bass
from concourse import mybir

F32, F16, I32 = mybir.dt.float32, mybir.dt.float16, mybir.dt.int32
ALU, ACT, AX = mybir.AluOpType, mybir.ActivationFunctionType, mybir.AxisListType

P = 128
B, S, D = 8, 512, 256
T = B * S
NT = T // P
KD = D // P
TPC = S // P
CH = B
NH = 16
E, HID, TOPK = 8, 512, 2
KH = HID // P
BLOCK = 256
SB = BLOCK // P
BLOCKS = (TOPK * T + E * (BLOCK - 1)) // BLOCK
SLOTS = BLOCKS * BLOCK
META = 4
ROW = 2 * D + 2 * META
EW = KD * 2 * HID + KH * D
PIECE = EW // 2
WSCALE = 16.0
EPS = 1e-5
MASKED = -3.0e38
ROWS_OUT = TOPK * T
NO_ROW = float(ROWS_OUT + 1)
N_SCATTERS = TOPK * NT


def repeat(eng, peeled, end, stride, body):
    for i in range(0, peeled, stride):
        body(i)
    with eng.Fori(peeled, end - stride + 1, stride) as i:
        body(i)


def build(nc, x, wq, wv, wg, wo, beta, ln_g, ln_b, router, w_exp, bias, out):
    ctx = ExitStack()
    with ctx:
        def sb(name, shape, dt=F32):
            return ctx.enter_context(nc.sbuf_tensor(name, shape, dt))

        def sem(name):
            return ctx.enter_context(nc.semaphore(name))

        slots_dram = nc.dram_tensor("slots_dram", (SLOTS, ROW // 2), I32).ap()
        y_dram = nc.dram_tensor("y_dram", (ROWS_OUT, D), F32).ap()

        w_raw = sb("w_raw", [P, E * EW])
        w_hi = w_raw[:, 0:E * EW // 2].bitcast(F16)
        w_lo = w_raw[:, E * EW // 2:E * EW].bitcast(F16)
        xst = w_raw[:, E * EW - NT * D:E * EW].rearrange("p (t d) -> p t d", d=D)
        rows_raw = sb("rows_raw", [P, NT * ROW // 2])
        rows16 = rows_raw[:, :].bitcast(F16).rearrange("p (t r) -> p t r", r=ROW)
        row_words = rows_raw[:, :].bitcast(I32).rearrange("p (t r) -> p t r", r=ROW // 2)
        rows32 = rows_raw[:, :].rearrange("p (t r) -> p t r", r=ROW // 2)
        xs_raw = sb("xs_raw", [P, NT * D])
        xnT = xs_raw[:, :].bitcast(F16).rearrange("p (c q n) -> p c q n", c=CH, q=2 * KD)
        s_all = xs_raw[:, :].rearrange("p (t d) -> p t d", d=D)
        work = sb("work", [P, NT * D])
        at = [0]

        def part(raw, words):
            at[0] += words
            return raw[:, at[0] - words:at[0]]

        states = part(work, KD * S).rearrange("p (m n) -> p m n", m=KD)
        z = part(work, KD * S).rearrange("p (j d) -> p j d", d=D)
        gate = part(work, KD * S).rearrange("p (m n) -> p m n", m=KD)
        w = part(work, KD * S).rearrange("p (m n) -> p m n", m=KD)
        p_hi = part(work, KD * S // 2).bitcast(F16).rearrange("p (m n) -> p m n", m=KD)
        p_lo = part(work, KD * S // 2).bitcast(F16).rearrange("p (m n) -> p m n", m=KD)
        wst = part(work, 2 * PIECE).rearrange("p (s n) -> p s n", s=2)
        assert at[0] <= NT * D
        x_again = work[:, :].rearrange("p (t d) -> p t d", d=D)
        wat_st = work[:, 0:4 * KD * D].rearrange("p (a k d) -> p a k d", a=4, k=KD)

        at[0] = 0
        slot_in = [part(rows_raw, SB * ROW // 2) for _ in range(2)]
        slot16 = [a.bitcast(F16).rearrange("p (s r) -> p s r", r=ROW) for a in slot_in]
        slot_words = [a.bitcast(I32).rearrange("p (s r) -> p s r", r=ROW // 2) for a in slot_in]
        slot32 = [a.rearrange("p (s r) -> p s r", r=ROW // 2) for a in slot_in]
        xT = [part(rows_raw, KD * BLOCK).bitcast(F16).rearrange("p (q n) -> p q n", q=2 * KD)
              for _ in range(2)]
        sil = [part(rows_raw, 2 * BLOCK).rearrange("p (m n) -> p m n", m=2) for _ in range(2)]
        g32 = [part(rows_raw, 2 * BLOCK).rearrange("p (m n) -> p m n", m=2) for _ in range(2)]
        g_hi = [part(rows_raw, KH * BLOCK // 2).bitcast(F16).rearrange("p (m n) -> p m n", m=KH)
                for _ in range(2)]
        g_lo = [part(rows_raw, KH * BLOCK // 2).bitcast(F16).rearrange("p (m n) -> p m n", m=KH)
                for _ in range(2)]
        ys = [part(rows_raw, SB * D).rearrange("p (s d) -> p s d", d=D) for _ in range(2)]
        assert at[0] <= NT * ROW // 2

        at[0] = 0
        y_in = [part(w_raw, TPC * TOPK * D).rearrange("p (t c d) -> p t c d", t=TPC, c=TOPK)
                for _ in range(2)]
        moe = [part(w_raw, TPC * D).rearrange("p (t d) -> p t d", d=D) for _ in range(2)]
        res = [part(w_raw, TPC * D).rearrange("p (t d) -> p t d", d=D) for _ in range(2)]

        at[0] = (E - 2) * EW // 2

        def routing(shape, dims, dt=F32, words=None):
            a = part(w_raw, (words or int(np.prod(shape))))
            a = a.bitcast(dt) if dt is not F32 else a
            return a.rearrange(f"p ({' '.join(dims)}) -> p {' '.join(dims)}", **dict(zip(dims, shape)))

        by_tile, by_expert = ((NT, E), "te"), ((E, NT), "et")
        e_of, lg_lo, lg, lg2, cand = [routing(*by_tile) for _ in range(5)]
        oh = [routing(*by_tile) for _ in range(TOPK)]
        seg, run, slot_of = [routing(*by_expert) for _ in range(3)]
        chosen = routing(*by_expert, dt=F16, words=E * NT // 2)
        blk_le = routing((BLOCKS, E), "be")
        assert at[0] <= E * EW // 2

        wat_hi = sb("wat_hi", [P, 4, KD, D], F16)
        wat_lo = sb("wat_lo", [P, 4, KD, D], F16)
        rt_st = sb("rt_st", [P, KD, E])
        rt = sb("rt", [P, KD, 2, E], F16)
        ident32 = sb("ident32", [P, P])
        ident16 = sb("ident16", [P, P], F16)
        before = sb("before", [P, P], F16)
        ones16 = sb("ones16", [P, P], F16)
        fill32 = sb("fill32", [P, ROW // 2])
        cols = sb("cols", [P, 4, KD])
        half_bias = sb("half_bias", [P, D])
        neg_half = sb("neg_half", [P, TPC])
        spare = sb("spare", [P, 6])
        bn = [sb(f"bn{i}", [P, TPC, 6]) for i in range(2)]
        mv = [sb(f"mv{i}", [P, TPC, 2]) for i in range(2)]
        stat = [sb(f"stat{i}", [P, 3, TPC]) for i in range(2)]
        tok_row = sb("tok_row", [P, NT])
        blk_of = sb("blk_of", [P, BLOCKS])
        top = [sb(f"top{c}", [P, NT]) for c in range(TOPK)]
        least = [sb(f"least{c}", [P, NT]) for c in range(TOPK)]
        th = sb("th", [P, NT])
        n_blk_i = sb("n_blk_i", [P, E], I32)
        n_blk = sb("n_blk", [P, E])
        blk_end = sb("blk_end", [P, E])
        blk_start = sb("blk_start", [P, E])
        blk_e = sb("blk_e", [P, BLOCKS])
        blk_off = sb("blk_off", [1, BLOCKS], I32)
        pos = [sb(f"pos{c}", [P, NT]) for c in range(TOPK)]
        pos_i = [sb(f"pos_i{c}", [P, NT], I32) for c in range(TOPK)]
        is_first = [sb(f"is_first{i}", [P, SB]) for i in range(2)]
        gate_c = [sb(f"gate_c{i}", [P, SB]) for i in range(2)]
        dest_f = [sb(f"dest_f{i}", [P, SB]) for i in range(2)]
        dest = [sb(f"dest{i}", [P, SB], I32) for i in range(2)]

        bankA, bankB, bankC, bankD = [
            ctx.enter_context(nc.psum_tensor(f"bank{n}", [P, 2, 512], F32)) for n in "ABCD"]
        AB = [bankA, bankB]
        AB16 = [b[:, :, :].bitcast(F16) for b in AB]
        logits_ps = bankD[:, 0, :].rearrange("p (t h e) -> p t h e", t=NT, h=2)
        rank_ps = bankD[:, 1, 0:E * NT].rearrange("p (e t) -> p e t", e=E)
        total_ps = bankD[:, 1, E * NT:2 * E * NT].rearrange("p (e t) -> p e t", e=E)
        D16 = [bankD[:, i, :].bitcast(F16).rearrange("p (q n) -> p q n", q=2 * KD)
               for i in range(2)]

        x_loaded = [sem(f"x_loaded{i}") for i in range(2)]
        rt_loaded, wat_loaded, cols_loaded, bias_loaded = map(
            sem, ("rt_loaded", "wat_loaded", "cols_loaded", "bias_loaded"))
        wst_loaded = [sem(f"wst_loaded{i}") for i in range(2)]
        consts, pool_step = sem("consts"), sem("pool_step")
        rt_hi, rt_split = sem("rt_hi"), sem("rt_split")
        lam_th, lam_ready, bias_halved = sem("lam_th"), sem("lam_ready"), sem("bias_halved")
        wat_scaled, wat_hi_ready, wat_lo_ready = map(
            sem, ("wat_scaled", "wat_hi_ready", "wat_lo_ready"))
        bn_done, x_var, x_rstd, x_norm, x_hi, x_lo = map(
            sem, ("bn_done", "x_var", "x_rstd", "x_norm", "x_hi", "x_lo"))
        xt_hi_ps, xt_lo_ps, xt_hi_sb, xt_lo_sb = map(
            sem, ("xt_hi_ps", "xt_lo_ps", "xt_hi_sb", "xt_lo_sb"))
        logits_done, lg_lo_ready, route_step, chosen_ready, ranks_done = map(
            sem, ("logits_done", "lg_lo_ready", "route_step", "chosen_ready", "ranks_done"))
        tops_ready, th_ready, routed = map(sem, ("tops_ready", "th_ready", "routed"))
        filled, rows_scattered = sem("filled"), sem("rows_scattered")
        v_ps, q_ps, g_ps, yt_ps, zt_ps, o_ps = map(
            sem, ("v_ps", "q_ps", "g_ps", "yt_ps", "zt_ps", "o_ps"))
        states_ready, prod_ready, ybn_done, y_var, y_rstd, z_ready = map(
            sem, ("states_ready", "prod_ready", "ybn_done", "y_var", "y_rstd", "z_ready"))
        w_ready, gate_ready, p_ready, p_hi_ready, p_lo_ready, s_ready = map(
            sem, ("w_ready", "gate_ready", "p_ready", "p_hi_ready", "p_lo_ready", "s_ready"))
        w_hi_ready, w_lo_ready = sem("w_hi_ready"), sem("w_lo_ready")
        x_again_loaded = sem("x_again_loaded")
        slot_loaded = [sem(f"slot_loaded{i}") for i in range(2)]
        slot_t_ps, slot_t_sb, h_ps, sil_ready, g_ready, g_hi_ready, g_split, y_ps, y_sb = map(
            sem, ("slot_t_ps", "slot_t_sb", "h_ps", "sil_ready", "g_ready", "g_hi_ready",
                  "g_split", "y_ps", "y_sb"))
        meta_ready = sem("meta_ready")
        y_scattered = [sem(f"y_scattered{i}") for i in range(2)]
        y_loaded = [sem(f"y_loaded{i}") for i in range(2)]
        moe_sum, moe_silu, gated, res_ready = map(
            sem, ("moe_sum", "moe_silu", "gated", "res_ready"))
        stored = [sem(f"stored{i}") for i in range(2)]

        x_v = x.rearrange("(t p) d -> p t d", p=P)
        out_v = out.rearrange("(t p) d -> p t d", p=P)
        y_v = y_dram.rearrange("(t p c) d -> p t c d", p=P, c=TOPK)
        slots_v = slots_dram.rearrange("(n p) r -> p n r", p=P)
        w_exp_v = w_exp.rearrange("p (n w) -> p n w", w=PIECE)

        block = ctx.enter_context(nc.Block())

        @block.sync
        def _(sp):
            def load_x(g):
                for i in range(2):
                    if not isinstance(g, int) or g >= 2:
                        sp.wait_ge(x_loaded[i], g * 8)
                    sp.dma_start(xst[:, bass.ds(g * TPC + i * TPC, TPC), :],
                                 x_v[:, bass.ds(g * TPC + i * TPC, TPC), :]).then_inc(x_loaded[i], 16)
            repeat(sp, 2, CH, 2, load_x)

            sp.wait_ge(consts, 1)
            sp.dma_start(slots_v, fill32[:, :].bitcast(I32).unsqueeze(1).to_broadcast([P, SLOTS // P, ROW // 2]))\
              .then_inc(filled, 16)

            def load_w(c):
                for i in range(2):
                    if isinstance(c, int) and c == 0:
                        sp.wait_ge(wat_lo_ready, 1)
                    else:
                        sp.wait_ge(w_lo_ready, c * 2 - 1 + i)
                    sp.dma_start(wst[:, i, :], w_exp_v[:, bass.ds(c * 2 + i, 1), :].rearrange(
                        "p a w -> p (a w)")).then_inc(wst_loaded[i], 16)
            repeat(sp, 1, CH, 1, load_w)

            sp.wait_ge(rows_scattered, 16 * N_SCATTERS)

            def load_slots(b, i):
                if not isinstance(b, int) or b >= 2:
                    sp.wait_ge(slot_t_ps, b - 1)
                    sp.wait_ge(meta_ready, b - 1)
                sp.dma_start(slot_words[i], slots_v[:, bass.ds(b * SB, SB), :]).then_inc(slot_loaded[i], 16)

            def two(b):
                load_slots(b, 0)
                load_slots(b + 1, 1)
            repeat(sp, 2, BLOCKS - 1, 2, two)
            load_slots(BLOCKS - 1, (BLOCKS - 1) % 2)

            sp.wait_ge(y_scattered[0], 16 * SB * ((BLOCKS + 1) // 2))
            sp.wait_ge(y_scattered[1], 16 * SB * (BLOCKS // 2))

            def load_y(g):
                for i in range(2):
                    if not isinstance(g, int) or g >= 2:
                        sp.wait_ge(moe_sum, g - 1 + i)
                    sp.dma_start(y_in[i], y_v[:, bass.ds(g * TPC + i * TPC, TPC), :, :])\
                      .then_inc(y_loaded[i], 16)
            repeat(sp, 2, CH, 2, load_y)
            for i in range(2):
                sp.wait_ge(stored[i], 16 * CH // 2)

        @block.gpsimd
        def _(pool):
            n = [0]

            def step(ins):
                n[0] += 1
                ins.then_inc(pool_step, 1)
                pool.wait_ge(pool_step, n[0])

            step(pool.memset(fill32[:, :], 0.0))
            step(pool.memset(fill32[:, D + META - 1:D + META], NO_ROW))
            pool.nop().then_inc(consts, 1)
            pool.memset(neg_half[:, :], -0.5)
            pool.memset(ident32[:, :], 0.0)
            pool.memset(before[:, :], 1.0)
            pool.memset(ones16[:, :], 1.0)
            step(pool.memset(ident16[:, :], 0.0))
            for m in (ident32, ident16):
                pool.affine_select(out=m[:, :], in_=m[:, :], compare_op=ALU.not_equal, fill=1.0,
                                   base=0, pattern=[[-1, P]], channel_multiplier=1)
            step(pool.affine_select(out=before[:, :], in_=before[:, :], compare_op=ALU.is_gt, fill=0.0,
                                    base=0, pattern=[[1, P]], channel_multiplier=-1))
            pool.nop().then_inc(consts, 1)

            def rstd(i, var_ready, count, out_ready):
                pool.wait_ge(var_ready, count)
                pool.tensor_scalar(stat[i][:, 0, :], mv[i][:, :, 1], EPS, None, ALU.add)
                step(pool.tensor_scalar(stat[i][:, 2, :], mv[i][:, :, 0], -1.0, None, ALU.mult))
                step(pool.tensor_tensor(stat[i][:, 1, :], stat[i][:, 0, :], neg_half[:, :], ALU.pow))
                pool.tensor_tensor(stat[i][:, 2, :], stat[i][:, 2, :], stat[i][:, 1, :],
                                   ALU.mult).then_inc(out_ready, 1)

            for g in range(CH):
                if g >= 2:
                    pool.wait_ge(x_norm, g - 1)
                rstd(g % 2, x_var, g + 1, x_rstd)
                if g == 0:
                    pool.iota(e_of[:, :, :], [[0, NT], [1, E]], base=0, channel_multiplier=0,
                              allow_small_or_imprecise_dtypes=True)
                    pool.iota(tok_row[:, :], [[2 * P, NT]], base=1, channel_multiplier=2,
                              allow_small_or_imprecise_dtypes=True)
                    pool.iota(blk_of[:, :], [[1, BLOCKS]], base=0, channel_multiplier=0,
                              allow_small_or_imprecise_dtypes=True)
                    step(pool.memset(seg[:, :, :], 1.0))
                    step(pool.memset(seg[:, :, 0:1], 0.0))
                    pool.nop().then_inc(consts, 1)
            pool.wait_ge(wat_hi_ready, 1)
            pool.tensor_tensor(wat_lo[:, :, :, :], wat_st, wat_hi[:, :, :, :], ALU.subtract)\
                .then_inc(wat_lo_ready, 1)

            pool.wait_ge(x_norm, CH)
            for c in range(CH):
                if c == 1:
                    pool.wait_ge(routed, 1)
                    pool.wait_ge(filled, 16)
                if c >= 1:
                    pool.wait_ge(z_ready, c)
                rstd(0, y_var, c + 1, y_rstd)
                if c == 0:
                    pool.wait_ge(routed, 1)
                    pool.wait_ge(filled, 16)
                for t in range(c * TPC, (c + 1) * TPC):
                    for k in range(TOPK):
                        pool.indirect_dma_start(
                            out=slots_dram, out_offset=bass.IndirectOffsetOnAxis(pos_i[k][:, t:t + 1], 0),
                            in_=row_words[:, t, :], in_offset=None,
                            bounds_check=SLOTS - 1, oob_is_err=False).then_inc(rows_scattered, 16)

            n_meta = n[0]

            def meta(b, i, first):
                pool.wait_ge(slot_loaded[i], b * 8 + 16 if i == 0 else b * 8 + 8)
                if not first:
                    pool.wait_ge(y_sb, b - 1)
                    pool.wait_ge(y_scattered[i], b * 16 if i == 0 else b * 16 - 16)
                e_b = blk_e[:, bass.ds(b, 1)].to_broadcast([P, SB])
                pool.tensor_tensor(is_first[i][:, :], slot32[i][:, :, D], e_b, ALU.subtract)\
                    .then_inc(pool_step, 1)
                pool.wait_ge(pool_step, b * 3 + n_meta + 1)
                pool.tensor_tensor(spare[:, i:i + 1], neg_half[:, 0:1], neg_half[:, 0:1], ALU.add)
                pool.tensor_scalar(is_first[i][:, :], is_first[i][:, :], 0.0, None, ALU.is_equal)\
                    .then_inc(pool_step, 1)
                pool.wait_ge(pool_step, b * 3 + n_meta + 2)
                pool.tensor_tensor(gate_c[i][:, :], slot32[i][:, :, D + 1], is_first[i][:, :], ALU.mult)
                pool.tensor_tensor(dest_f[i][:, :], slot32[i][:, :, D + 3], is_first[i][:, :], ALU.subtract)\
                    .then_inc(pool_step, 1)
                pool.wait_ge(pool_step, b * 3 + n_meta + 3)
                pool.tensor_tensor(gate_c[i][:, :], gate_c[i][:, :], slot32[i][:, :, D + 2], ALU.add)
                pool.tensor_copy(dest[i][:, :], dest_f[i][:, :]).then_inc(meta_ready, 1)

            def scatter_y(b, i):
                pool.wait_ge(y_sb, b + 1)
                pool.wait_ge(meta_ready, b + 1)
                pool.tensor_tensor(spare[:, 2 + i:3 + i], neg_half[:, 0:1], neg_half[:, 0:1], ALU.add)
                for s in range(SB):
                    pool.indirect_dma_start(
                        out=y_dram, out_offset=bass.IndirectOffsetOnAxis(dest[i][:, s:s + 1], 0),
                        in_=ys[i][:, s, :], in_offset=None,
                        bounds_check=ROWS_OUT - 1, oob_is_err=False).then_inc(y_scattered[i], 16)

            pool.wait_ge(rows_scattered, 16 * N_SCATTERS)
            meta(0, 0, True)
            meta(1, 1, True)
            scatter_y(0, 0)
            with pool.Fori(2, BLOCKS - 2, 2) as b:
                meta(b, 0, False)
                scatter_y(b - 1, 1)
                meta(b + 1, 1, False)
                scatter_y(b, 0)
            meta(BLOCKS - 1, 0, False)
            scatter_y(BLOCKS - 2, 1)
            scatter_y(BLOCKS - 1, 0)

            pool.wait_ge(x_again_loaded, 16)

            def add_x(g):
                for i in range(2):
                    pool.wait_ge(gated, g + i + 1)
                    pool.tensor_tensor(res[i], res[i], x_again[:, bass.ds(g * TPC + i * TPC, TPC), :],
                                       ALU.add).then_inc(res_ready, 1)
            repeat(pool, 0, CH, 2, add_x)

        @block.scalar
        def _(act):
            act.dma_start(rt_st[:, :, :], router).then_inc(rt_loaded, 16)
            for n, a in enumerate((beta, ln_g, ln_b)):
                act.dma_start(cols[:, n, :], a).then_inc(cols_loaded, 16)
            act.dma_start(half_bias[:, :], bias).then_inc(bias_loaded, 16)
            for n, a in enumerate((wq, wv, wg, wo)):
                act.dma_start(wat_st[:, n, :, :], a.rearrange("(k p) d -> p k d", p=P))\
                   .then_inc(wat_loaded, 16)
            act.wait_ge(rt_loaded, 16)
            act.activation(rt[:, :, 0, :], rt_st[:, :, :], ACT.Copy, scale=WSCALE).then_inc(rt_hi, 1)
            act.wait_ge(cols_loaded, 48)
            act.activation(cols[:, 3, :], cols[:, 0, :], ACT.Tanh, scale=0.5).then_inc(lam_th, 1)
            act.wait_ge(bias_loaded, 16)
            act.activation(half_bias[:, :], half_bias[:, :], ACT.Copy, scale=0.5).then_inc(bias_halved, 1)

            def norm_x(g, i):
                act.wait_ge(x_rstd, g + 1)
                for j in range(TPC):
                    xt = xst[:, bass.ds(g * TPC + j, 1), :].rearrange("p a d -> p (a d)")
                    last = act.activation(xt, xt, ACT.Identity, bias=stat[i][:, 2, j:j + 1],
                                          scale=stat[i][:, 1, j:j + 1])
                last.then_inc(x_norm, 1)
                act.wait_ge(x_norm, g + 1)
                act.activation(rows16[:, bass.ds(g * TPC, TPC), 0:D], xst[:, bass.ds(g * TPC, TPC), :],
                               ACT.Copy).then_inc(x_hi, 1)

            def copy_xt_lo(g, i):
                act.wait_ge(xt_lo_ps, g + 1)
                act.activation(xnT[:, bass.ds(g, 1), KD:2 * KD, :].rearrange("p a q n -> p (a q n)"),
                               AB16[i][:, 1, :], ACT.Copy).then_inc(xt_lo_sb, 1)

            norm_x(0, 0)
            norm_x(1, 1)
            copy_xt_lo(0, 0)
            with act.Fori(2, CH - 1, 2) as g:
                norm_x(g, 0)
                copy_xt_lo(g - 1, 1)
                norm_x(g + 1, 1)
                copy_xt_lo(g, 0)
            copy_xt_lo(CH - 1, 1)

            act.wait_ge(logits_done, 1)
            act.activation(lg_lo[:, :, :], logits_ps[:, :, 1, :], ACT.Copy).then_inc(lg_lo_ready, 1)
            act.wait_ge(wat_loaded, 64)
            act.activation(wat_st, wat_st, ACT.Copy, scale=WSCALE).then_inc(wat_scaled, 1)
            act.wait_ge(wat_scaled, 1)
            act.activation(wat_hi[:, :, :, :], wat_st, ACT.Copy).then_inc(wat_hi_ready, 1)
            act.wait_ge(tops_ready, 1)
            act.activation(th[:, :], th[:, :], ACT.Tanh, scale=0.5 / WSCALE).then_inc(th_ready, 1)

            def affine(c):
                act.wait_ge(zt_ps, c)
                if not isinstance(c, int) or c >= 2:
                    act.wait_ge(p_lo_ready, c - 1)
                for m in range(KD):
                    last = act.activation(w[:, m, :], bankA[:, m, :], ACT.Identity,
                                          bias=cols[:, 2, m:m + 1], scale=cols[:, 1, m:m + 1])
                last.then_inc(w_ready, 1)

            def split_p(c):
                act.wait_ge(p_ready, c)
                if not isinstance(c, int) or c >= 2:
                    act.wait_ge(o_ps, c - 1)
                act.activation(p_hi, w, ACT.Copy).then_inc(p_hi_ready, 1)

            def keep_s(c):
                act.wait_ge(o_ps, c)
                act.activation(s_all[:, bass.ds(c * TPC - TPC, TPC), :].rearrange("p t d -> p (t d)"),
                               bankC[:, :, :].rearrange("p a b -> p (a b)"), ACT.Copy,
                               scale=1.0 / WSCALE).then_inc(s_ready, 1)

            def recur(c):
                later = not isinstance(c, int) or c >= 1
                if later:
                    affine(c)
                    split_p(c)
                act.wait_ge(g_ps, c + 1)
                if later:
                    act.wait_ge(p_ready, c)
                act.activation(gate, bankC[:, :, :], ACT.Silu, scale=1.0 / WSCALE).then_inc(gate_ready, 1)
                act.wait_ge(y_rstd, c + 1)
                for j in range(TPC):
                    last = act.activation(z[:, j, :], bankB[:, j // 2, j % 2 * D:j % 2 * D + D],
                                          ACT.Identity, bias=stat[0][:, 2, j:j + 1],
                                          scale=stat[0][:, 1, j:j + 1])
                last.then_inc(z_ready, 1)
                for i in range(2):
                    act.wait_ge(wst_loaded[i], c * 16 + 16)
                    act.activation(w_hi[:, bass.ds(c * EW + i * PIECE, PIECE)], wst[:, i, :], ACT.Copy,
                                   scale=WSCALE).then_inc(w_hi_ready, 1)
                if later:
                    keep_s(c)
            repeat(act, 1, CH, 1, recur)
            affine(CH)
            split_p(CH)
            keep_s(CH)
            act.wait_ge(w_lo_ready, 2 * E)
            act.dma_start(x_again, x_v).then_inc(x_again_loaded, 16)

            def halves(b, i, first):
                for j in range(2):
                    act.wait_ge(h_ps, b * 2 + j + 1)
                    if first < 1:
                        act.wait_ge(g_ready, b * 2 - 1 + j)
                    act.activation(sil[j], AB[j][:, :, 0:BLOCK], ACT.Silu,
                                   scale=1.0 / WSCALE).then_inc(sil_ready, 1)
                    act.wait_ge(g_ready, b * 2 + j + 1)
                    if first < 0:
                        act.wait_ge(y_ps, b - 1)
                    act.activation(g_hi[i][:, 2 * j:2 * j + 2, :], g32[j], ACT.Copy)\
                       .then_inc(g_hi_ready, 1)

            act.wait_ge(rows_scattered, 16 * N_SCATTERS)
            halves(0, 0, 1)
            halves(1, 1, 0)
            with act.Fori(2, BLOCKS - 2, 2) as b:
                halves(b, 0, -1)
                halves(b + 1, 1, -1)
            halves(BLOCKS - 1, 0, -1)

            def silu_moe(g):
                for i in range(2):
                    act.wait_ge(moe_sum, g + i + 1)
                    act.activation(moe[i], moe[i], ACT.Silu).then_inc(moe_silu, 1)
                    act.wait_ge(res_ready, g + i + 1)
                    act.dma_start(out_v[:, bass.ds(g * TPC + i * TPC, TPC), :], res[i])\
                       .then_inc(stored[i], 16)
            repeat(act, 0, CH, 2, silu_moe)

        @block.vector
        def _(dve):
            n = [0]

            def step(ins):
                n[0] += 1
                ins.then_inc(route_step, 1)
                dve.wait_ge(route_step, n[0])

            dve.wait_ge(rt_hi, 1)
            dve.scalar_tensor_tensor(rt[:, :, 1, :], rt_st[:, :, :], WSCALE, rt[:, :, 0, :],
                                     ALU.mult, ALU.subtract).then_inc(rt_split, 1)

            def stats_x(g, i):
                dve.wait_ge(x_loaded[i], (g * 8 + 16) if i == 0 else (g * 8 + 8))
                later = not isinstance(g, int) or g >= 2
                if later:
                    dve.wait_ge(x_var, g - 1)
                for j in range(TPC):
                    last = dve.bn_stats(bn[i][:, j, :],
                                        xst[:, bass.ds(g * TPC + j, 1), :].rearrange("p a d -> p (a d)"))
                last.then_inc(bn_done, 1)
                dve.wait_ge(bn_done, g + 1)
                if later:
                    dve.wait_ge(x_rstd, g - 1)
                dve.memset(spare[:, 4 + i:5 + i], 0.0)
                for j in range(TPC):
                    last = dve.bn_aggr(mv[i][:, j, :], bn[i][:, j, :])
                last.then_inc(x_var, 1)

            def low_x(g, i):
                dve.wait_ge(x_hi, g + 1)
                tiles = bass.ds(g * TPC, TPC)
                dve.tensor_tensor(rows16[:, tiles, D:2 * D], xst[:, tiles, :], rows16[:, tiles, 0:D],
                                  ALU.subtract).then_inc(x_lo, 1)
                dve.wait_ge(xt_hi_ps, g + 1)
                dve.tensor_copy(xnT[:, bass.ds(g, 1), 0:KD, :].rearrange("p a q n -> p (a q n)"),
                                AB16[i][:, 0, :]).then_inc(xt_hi_sb, 1)

            stats_x(0, 0)
            stats_x(1, 1)
            low_x(0, 0)
            with dve.Fori(2, CH - 1, 2) as g:
                stats_x(g, 0)
                low_x(g - 1, 1)
                stats_x(g + 1, 1)
                low_x(g, 0)
            low_x(CH - 1, 1)

            def tiles_of(a):
                return a[:, :].unsqueeze(2).to_broadcast([P, NT, E])

            dve.wait_ge(lg_lo_ready, 1)
            dve.wait_ge(consts, 3)
            step(dve.tensor_tensor(lg[:, :, :], logits_ps[:, :, 0, :], lg_lo[:, :, :], ALU.add))
            src = lg
            for c in range(TOPK):
                step(dve.tensor_reduce(top[c][:, :], src[:, :, :], AX.X, ALU.max))
                step(dve.tensor_tensor(cand[:, :, :], src[:, :, :], tiles_of(top[c]), ALU.is_equal))
                step(dve.scalar_tensor_tensor(cand[:, :, :], cand[:, :, :], -16.0, e_of[:, :, :],
                                              ALU.mult, ALU.add))
                step(dve.tensor_reduce(least[c][:, :], cand[:, :, :], AX.X, ALU.min))
                step(dve.tensor_tensor(oh[c][:, :, :], cand[:, :, :], tiles_of(least[c]), ALU.is_equal))
                if c == 0:
                    step(dve.scalar_tensor_tensor(lg2[:, :, :], oh[0][:, :, :], MASKED, lg[:, :, :],
                                                  ALU.mult, ALU.add))
                    src = lg2
            dve.tensor_tensor(chosen[:, :, :].rearrange("p e t -> p t e"), oh[0][:, :, :], oh[1][:, :, :],
                              ALU.add).then_inc(chosen_ready, 1)
            dve.tensor_tensor(th[:, :], top[0][:, :], top[1][:, :], ALU.subtract).then_inc(tops_ready, 1)

            dve.wait_ge(ranks_done, 1)
            flat = "p e t -> p (e t)"
            step(dve.tensor_tensor_scan(run[:, :, :].rearrange(flat), seg[:, :, :].rearrange(flat),
                                        total_ps.rearrange(flat), 0.0, ALU.mult, ALU.add))
            n_e = run[:, :, NT - 1]
            step(dve.tensor_scalar(n_blk_i[:, :], n_e, float(BLOCK - 1), None, ALU.add))
            step(dve.tensor_single_scalar(n_blk_i[:, :], n_blk_i[:, :], BLOCK.bit_length() - 1,
                                          ALU.logical_shift_right))
            step(dve.tensor_copy(n_blk[:, :], n_blk_i[:, :]))
            step(dve.tensor_tensor_scan(blk_end[:, :], seg[:, 0, 1:E + 1], n_blk[:, :], 0.0,
                                        ALU.mult, ALU.add))
            step(dve.tensor_tensor(blk_start[:, :], blk_end[:, :], n_blk[:, :], ALU.subtract))
            step(dve.tensor_tensor(slot_of[:, :, :], run[:, :, :], total_ps, ALU.subtract))
            step(dve.tensor_tensor(slot_of[:, :, :], slot_of[:, :, :], rank_ps, ALU.add))
            step(dve.scalar_tensor_tensor(slot_of[:, :, :],
                                          blk_start[:, :].unsqueeze(2).to_broadcast([P, E, NT]),
                                          float(BLOCK), slot_of[:, :, :], ALU.mult, ALU.add))
            for c in range(TOPK):
                step(dve.tensor_tensor(cand[:, :, :], oh[c][:, :, :],
                                       slot_of[:, :, :].rearrange("p e t -> p t e"), ALU.mult))
                step(dve.tensor_reduce(pos[c][:, :], cand[:, :, :], AX.X, ALU.add))
                dve.tensor_copy(pos_i[c][:, :], pos[c][:, :])
            dve.tensor_copy(rows32[:, :, D], least[0][:, :])
            dve.tensor_copy(rows32[:, :, D + 3], tok_row[:, :])
            dve.wait_ge(th_ready, 1)
            dve.tensor_scalar(rows32[:, :, D + 1], th[:, :], 1.0 / WSCALE, None, ALU.mult)
            dve.tensor_scalar(rows32[:, :, D + 2], th[:, :], -0.5 / WSCALE, 0.5 / WSCALE, ALU.mult, ALU.add)\
               .then_inc(routed, 1)
            step(dve.tensor_tensor(blk_le[:, :, :], blk_end[:, :].unsqueeze(1).to_broadcast([P, BLOCKS, E]),
                                   blk_of[:, :].unsqueeze(2).to_broadcast([P, BLOCKS, E]), ALU.is_le))
            step(dve.tensor_reduce(blk_e[:, :], blk_le[:, :, :], AX.X, ALU.add))
            step(dve.tensor_single_scalar(blk_e[:, :], blk_e[:, :], float(E - 1), ALU.min))
            step(dve.tensor_single_scalar(blk_off[:, :], blk_e[0:1, :], float(EW), ALU.mult))
            step(dve.tensor_single_scalar(blk_e[:, :], blk_e[:, :], -16.0, ALU.add))
            dve.wait_ge(lam_th, 1)
            dve.tensor_scalar(cols[:, 3, :], cols[:, 3, :], 0.5, 0.5, ALU.mult, ALU.add)\
               .then_inc(lam_ready, 1)
            dve.wait_ge(lam_ready, 1)

            def recur(c):
                later = not isinstance(c, int) or c >= 1
                dve.wait_ge(v_ps, c + 1)
                if later:
                    dve.wait_ge(yt_ps, c)
                else:
                    dve.wait_ge(wat_lo_ready, 1)
                for m in range(KD):
                    last = dve.tensor_tensor_scan(states[:, m, :], cols[:, 3, m:m + 1].to_broadcast([P, S]),
                                                  bankA[:, m, :], 0.0, ALU.mult, ALU.add)
                last.then_inc(states_ready, 1)
                dve.wait_ge(q_ps, c + 1)
                dve.wait_ge(states_ready, c + 1)
                dve.scalar_tensor_tensor(states, bankB[:, :, :], 1.0 / WSCALE ** 2, states, ALU.mult, ALU.mult)\
                   .then_inc(prod_ready, 1)
                if later:
                    times_gate(c)
                dve.wait_ge(yt_ps, c + 1)
                if later:
                    dve.wait_ge(y_var, c)
                else:
                    dve.wait_ge(x_var, CH)
                for j in range(TPC):
                    last = dve.bn_stats(bn[0][:, j, :], bankB[:, j // 2, j % 2 * D:j % 2 * D + D])
                last.then_inc(ybn_done, 1)
                dve.wait_ge(ybn_done, c + 1)
                if later:
                    dve.wait_ge(y_rstd, c)
                dve.memset(spare[:, 4:5], 0.0)
                for j in range(TPC):
                    last = dve.bn_aggr(mv[0][:, j, :], bn[0][:, j, :])
                last.then_inc(y_var, 1)
                for i in range(2):
                    dve.wait_ge(w_hi_ready, c * 2 + i + 1)
                    piece = bass.ds(c * EW + i * PIECE, PIECE)
                    dve.scalar_tensor_tensor(w_lo[:, piece], wst[:, i, :], WSCALE, w_hi[:, piece],
                                             ALU.mult, ALU.subtract).then_inc(w_lo_ready, 1)

            def times_gate(c):
                dve.wait_ge(w_ready, c)
                dve.wait_ge(gate_ready, c)
                dve.tensor_tensor(w, w, gate, ALU.mult).then_inc(p_ready, 1)
                dve.wait_ge(p_hi_ready, c)
                dve.tensor_tensor(p_lo, w, p_hi, ALU.subtract).then_inc(p_lo_ready, 1)
            repeat(dve, 1, CH, 1, recur)
            times_gate(CH)

            dve.wait_ge(rows_scattered, 16 * N_SCATTERS)
            dve.wait_ge(bias_halved, 1)

            def copy_xt(b, i, first):
                dve.wait_ge(slot_t_ps, b + 1)
                if not first:
                    dve.wait_ge(h_ps, b * 2 - 2)
                dve.tensor_copy(xT[i], D16[i]).then_inc(slot_t_sb, 1)

            def half(b, i, j):
                dve.wait_ge(sil_ready, b * 2 + j + 1)
                dve.scalar_tensor_tensor(g32[j], sil[j], 1.0 / WSCALE, AB[j][:, :, BLOCK:2 * BLOCK],
                                         ALU.mult, ALU.mult).then_inc(g_ready, 1)
                dve.wait_ge(g_hi_ready, b * 2 + j + 1)
                dve.tensor_tensor(g_lo[i][:, 2 * j:2 * j + 2, :], g32[j], g_hi[i][:, 2 * j:2 * j + 2, :],
                                  ALU.subtract).then_inc(g_split, 1)

            def gate_y(b, i, first):
                dve.wait_ge(y_ps, b + 1)
                dve.wait_ge(meta_ready, b + 1)
                if not first:
                    dve.wait_ge(y_scattered[i], b * 16 if i == 0 else b * 16 - 16)
                for s in range(SB):
                    last = dve.scalar_tensor_tensor(ys[i][:, s, :], bankC[:, i, s * D:s * D + D],
                                                    gate_c[i][:, s:s + 1], half_bias[:, :],
                                                    ALU.mult, ALU.add)
                last.then_inc(y_sb, 1)

            def blocks(b, i, first, last=False):
                half(b, i, 0)
                if not last:
                    copy_xt(b + 1, 1 - i, first)
                half(b, i, 1)
            copy_xt(0, 0, True)
            blocks(0, 0, True)
            blocks(1, 1, False)
            gate_y(0, 0, True)
            with dve.Fori(2, BLOCKS - 2, 2) as b:
                blocks(b, 0, False)
                gate_y(b - 1, 1, False)
                blocks(b + 1, 1, False)
                gate_y(b, 0, False)
            blocks(BLOCKS - 1, 0, False, True)
            gate_y(BLOCKS - 2, 1, False)
            gate_y(BLOCKS - 1, 0, False)

            def finish(g):
                for i in range(2):
                    later = not isinstance(g, int) or g >= 2
                    dve.wait_ge(y_loaded[i], g * 8 + 16)
                    dve.tensor_tensor(moe[i], y_in[i][:, :, 0, :], y_in[i][:, :, 1, :], ALU.add)\
                       .then_inc(moe_sum, 1)
                    dve.wait_ge(moe_silu, g + i + 1)
                    if later:
                        dve.wait_ge(stored[i], g * 8)
                    dve.tensor_tensor(res[i], moe[i], s_all[:, bass.ds(g * TPC + i * TPC, TPC), :],
                                      ALU.mult).then_inc(gated, 1)
            repeat(dve, 2, CH, 2, finish)

        @block.tensor
        def _(pe):
            def three(out_ap, pairs, hi_l, lo_l, hi_r, lo_r):
                todo = [(a(k), b(k)) for k in pairs for a, b in ((hi_l, hi_r), (hi_l, lo_r), (lo_l, hi_r))]
                for n, (lhsT, rhs) in enumerate(todo):
                    last = pe.matmul(out_ap, lhsT, rhs, start=(n == 0), stop=(n == len(todo) - 1))
                return last

            pe.wait_ge(consts, 2)

            def transpose_x(g, i):
                for h, (ready, done, free) in enumerate(((x_hi, xt_hi_ps, xt_hi_sb),
                                                         (x_lo, xt_lo_ps, xt_lo_sb))):
                    pe.wait_ge(ready, g + 1)
                    if not isinstance(g, int) or g >= 2:
                        pe.wait_ge(free, g - 1)
                    for j in range(TPC):
                        for k in range(KD):
                            src = rows16[:, bass.ds(g * TPC + j, 1), h * D + k * P:h * D + k * P + P]
                            last = pe.transpose(AB16[i][:, h, k * S + j * P:k * S + j * P + P],
                                                src.rearrange("p a d -> p (a d)"), ident16[:, :])
                    last.then_inc(done, 1)

            def route_x(g):
                pe.wait_ge(xt_hi_sb, g + 1)
                pe.wait_ge(xt_lo_sb, g + 1)
                for j in range(TPC):
                    dst = logits_ps[:, bass.ds(g * TPC + j, 1), :, :].rearrange("p a h e -> p (a h e)")
                    for q in range(2 * KD):
                        last = pe.matmul(dst, xnT[:, bass.ds(g, 1), q, j * P:j * P + P].rearrange(
                            "p a n -> p (a n)"), rt[:, q % KD, :, :].rearrange("p h e -> p (h e)"),
                            start=(q == 0), stop=(q == 2 * KD - 1))
                return last

            transpose_x(0, 0)
            transpose_x(1, 1)
            pe.wait_ge(rt_split, 1)
            route_x(0)
            with pe.Fori(2, CH - 1, 2) as g:
                transpose_x(g, 0)
                route_x(g - 1)
                transpose_x(g + 1, 1)
                route_x(g)
            route_x(CH - 1).then_inc(logits_done, 1)

            def project(bank, a, c):
                for m in range(KD):
                    last = three(bank[:, m, :], range(KD),
                                 lambda k: wat_hi[:, a, k, m * P:m * P + P],
                                 lambda k: wat_lo[:, a, k, m * P:m * P + P],
                                 lambda k: xnT[:, bass.ds(c, 1), k, :].rearrange("p a n -> p (a n)"),
                                 lambda k: xnT[:, bass.ds(c, 1), KD + k, :].rearrange("p a n -> p (a n)"))
                return last

            def transpose_z(c):
                pe.wait_ge(z_ready, c)
                for j in range(TPC):
                    for m in range(KD):
                        last = pe.transpose(bankA[:, m, j * P:j * P + P], z[:, j, m * P:m * P + P],
                                            ident32[:, :])
                last.then_inc(zt_ps, 1)

            def project_out(c):
                pe.wait_ge(p_lo_ready, c)
                for j in range(TPC):
                    last = three(bankC[:, j // 2, j % 2 * D:j % 2 * D + D], range(KD),
                                 lambda k: p_hi[:, k, j * P:j * P + P],
                                 lambda k: p_lo[:, k, j * P:j * P + P],
                                 lambda k: wat_hi[:, 3, k, :],
                                 lambda k: wat_lo[:, 3, k, :])
                last.then_inc(o_ps, 1)

            pe.wait_ge(wat_lo_ready, 1)

            def recur(c):
                later = not isinstance(c, int) or c >= 1
                if not isinstance(c, int) or c >= 2:
                    pe.wait_ge(w_ready, c - 1)
                project(bankA, 1, c).then_inc(v_ps, 1)
                if later:
                    pe.wait_ge(z_ready, c)
                project(bankB, 0, c).then_inc(q_ps, 1)
                if later:
                    pe.wait_ge(states_ready, c + 1)
                    transpose_z(c)
                if not isinstance(c, int) or c >= 2:
                    pe.wait_ge(s_ready, c - 1)
                project(bankC, 2, c).then_inc(g_ps, 1)
                if not later:
                    pe.wait_ge(chosen_ready, 1)
                    chosen_v = chosen[:, :, :].rearrange("p e t -> p (e t)")
                    pe.matmul(rank_ps.rearrange("p e t -> p (e t)"), before[:, :], chosen_v,
                              start=True, stop=True)
                    pe.matmul(total_ps.rearrange("p e t -> p (e t)"), ones16[:, :], chosen_v,
                              start=True, stop=True).then_inc(ranks_done, 1)
                pe.wait_ge(prod_ready, c + 1)
                for j in range(TPC):
                    for m in range(KD):
                        last = pe.transpose(bankB[:, j // 2, j % 2 * D + m * P:j % 2 * D + m * P + P],
                                            states[:, m, j * P:j * P + P], ident32[:, :])
                last.then_inc(yt_ps, 1)
                if later:
                    pe.wait_ge(gate_ready, c + 1)
                    project_out(c)
            repeat(pe, 1, CH, 1, recur)
            transpose_z(CH)
            pe.wait_ge(s_ready, CH - 1)
            project_out(CH)

            def weights_at(b):
                return pe.value_load(blk_off[0:1, bass.ds(b, 1)], min_val=0, max_val=(E - 1) * EW)

            def transpose_slots(b, i, first):
                pe.wait_ge(slot_loaded[i], b * 8 + 16 if i == 0 else b * 8 + 8)
                if not first:
                    pe.wait_ge(slot_t_sb, b - 1)
                for q in range(2 * KD):
                    for s in range(SB):
                        last = pe.transpose(D16[i][:, q, s * P:s * P + P],
                                            slot16[i][:, s, q * P:q * P + P], ident16[:, :])
                last.then_inc(slot_t_ps, 1)

            def hidden(b, i, j, off, first):
                if not first:
                    pe.wait_ge(g_ready, b * 2 - 1 + j)
                for m in (2 * j, 2 * j + 1):
                    for half in range(2):
                        col = half * HID + m * P
                        last = three(AB[j][:, m % 2, half * BLOCK:half * BLOCK + BLOCK], range(KD),
                                     lambda k: w_hi[:, bass.ds(off + (k * 2 * HID + col), P)],
                                     lambda k: w_lo[:, bass.ds(off + (k * 2 * HID + col), P)],
                                     lambda k: xT[i][:, k, :],
                                     lambda k: xT[i][:, KD + k, :])
                last.then_inc(h_ps, 1)

            def outputs(b, i, off, first):
                pe.wait_ge(g_split, b * 2 + 2)
                if not first:
                    pe.wait_ge(y_sb, b - 1)
                for s in range(SB):
                    last = three(bankC[:, i, s * D:s * D + D], range(KH),
                                 lambda k: g_hi[i][:, k, s * P:s * P + P],
                                 lambda k: g_lo[i][:, k, s * P:s * P + P],
                                 lambda k: w_hi[:, bass.ds(off + (KD * 2 * HID + k * D), D)],
                                 lambda k: w_lo[:, bass.ds(off + (KD * 2 * HID + k * D), D)])
                last.then_inc(y_ps, 1)

            def one_block(b, i, first=False, last=False, second=False, third=False):
                off = weights_at(b)
                pe.wait_ge(slot_t_sb, b + 1)
                hidden(b, i, 0, off, first)
                if not last:
                    transpose_slots(b + 1, 1 - i, first)
                hidden(b, i, 1, off, first)
                if not first:
                    outputs(b - 1, 1 - i, weights_at(b - 1), second or third)

            pe.wait_ge(w_lo_ready, 2 * E)
            pe.wait_ge(s_ready, CH)
            transpose_slots(0, 0, True)
            one_block(0, 0, first=True)
            one_block(1, 1, second=True)
            with pe.Fori(2, BLOCKS - 2, 2) as b:
                one_block(b, 0)
                one_block(b + 1, 1)
            one_block(BLOCKS - 1, 0, last=True)
            outputs(BLOCKS - 1, 0, weights_at(BLOCKS - 1), False)


_OUT_SHAPE = (B, S, D)


def kernel(L0_attn_x, L0_attn_Wq, L0_attn_Wv, L0_attn_Wg, L0_attn_Wo, L0_attn_beta, L0_attn_ln_g,
           L0_attn_ln_b, L0_ffn_router_weight, L0_ffn_w_in, L0_ffn_w_out, L0_ffn_bias):
    import concourse.bacc as bacc
    from concourse.bass_utils import run_bass_kernel_spmd

    def by_partition(a):
        return np.ascontiguousarray(a.reshape(KD, P, -1).transpose(1, 0, 2))

    def column(a):
        return np.ascontiguousarray(a.reshape(KD, P).T)

    w_in = np.asarray(L0_ffn_w_in).reshape(E, 2 * HID, KD, P).transpose(3, 0, 2, 1)
    w_out = np.asarray(L0_ffn_w_out).reshape(E, D, KH, P).transpose(3, 0, 2, 1)
    w_exp = np.concatenate([w_in.reshape(P, E, -1), w_out.reshape(P, E, -1)], axis=2).reshape(P, E * EW)
    arrays = {
        "x": np.asarray(L0_attn_x).reshape(T, D),
        "wq": np.asarray(L0_attn_Wq), "wv": np.asarray(L0_attn_Wv),
        "wg": np.asarray(L0_attn_Wg), "wo": np.asarray(L0_attn_Wo),
        "beta": column(np.repeat(np.asarray(L0_attn_beta), D // NH)),
        "ln_g": column(np.asarray(L0_attn_ln_g)), "ln_b": column(np.asarray(L0_attn_ln_b)),
        "router": by_partition(np.asarray(L0_ffn_router_weight).T),
        "w_exp": w_exp,
        "bias": np.broadcast_to(np.asarray(L0_ffn_bias), (P, D)),
    }
    arrays = {f"{k}_in": np.ascontiguousarray(v) for k, v in arrays.items()}
    nc = bacc.Bacc("TRN2", target_bir_lowering=False, num_devices=1)
    args = [nc.dram_tensor(k, v.shape, mybir.dt.from_np(v.dtype), kind="ExternalInput").ap()
            for k, v in arrays.items()]
    out = nc.dram_tensor("out", (T, D), F32, kind="ExternalOutput").ap()
    build(nc, *args, out)
    r = run_bass_kernel_spmd(nc, [arrays], core_ids=[0])
    return r.results[0]["out"].reshape(_OUT_SHAPE)
```

```python
from contextlib import ExitStack

import numpy as np

import concourse.bass as bass
from concourse import mybir

F32, F16, I32 = mybir.dt.float32, mybir.dt.float16, mybir.dt.int32
ALU, ACT, AX = mybir.AluOpType, mybir.ActivationFunctionType, mybir.AxisListType

P = 128
B, S, D = 8, 512, 256
T = B * S
NT = T // P
KD = D // P
TPC = S // P
CH = B
NH = 16
E, HID, TOPK = 8, 512, 2
KH = HID // P
BLOCK = 256
SB = BLOCK // P
BLOCKS = (TOPK * T + E * (BLOCK - 1)) // BLOCK
SLOTS = BLOCKS * BLOCK
META = 4
ROW = 2 * D + 2 * META
EW = KD * 2 * HID + KH * D
EARLY = CH - 1
CONVERT = 6
PIECES = 4
PIECE = E * EW // (CONVERT * PIECES)
WSCALE = 16.0
EPS = 1e-5
MASKED = -3.0e38
ROWS_OUT = TOPK * T
NO_ROW = float(ROWS_OUT + 1)
PADS = (SLOTS - TOPK * T) // P
N_SCATTERS = TOPK * NT + PADS


def repeat(eng, peeled, end, stride, body):
    for i in range(0, peeled, stride):
        body(i)
    with eng.Fori(peeled, end - stride + 1, stride) as i:
        body(i)


def build(nc, x, wq, wv, wg, wo, beta, ln_g, ln_b, router, w_exp, bias, out):
    ctx = ExitStack()
    with ctx:
        def sb(name, shape, dt=F32):
            return ctx.enter_context(nc.sbuf_tensor(name, shape, dt))

        def sem(name):
            return ctx.enter_context(nc.semaphore(name))

        slots_dram = nc.dram_tensor("slots_dram", (SLOTS, ROW // 2), I32).ap()
        y_dram = nc.dram_tensor("y_dram", (ROWS_OUT, D), F32).ap()

        w_raw = sb("w_raw", [P, E * EW])
        w_hi = w_raw[:, 0:E * EW // 2].bitcast(F16)
        w_lo = w_raw[:, E * EW // 2:E * EW].bitcast(F16)
        xst = w_raw[:, E * EW - NT * D:E * EW].rearrange("p (t d) -> p t d", d=D)
        rows_raw = sb("rows_raw", [P, NT * ROW // 2])
        rows16 = rows_raw[:, :].bitcast(F16).rearrange("p (t r) -> p t r", r=ROW)
        row_words = rows_raw[:, :].bitcast(I32).rearrange("p (t r) -> p t r", r=ROW // 2)
        rows32 = rows_raw[:, :].rearrange("p (t r) -> p t r", r=ROW // 2)
        xs_raw = sb("xs_raw", [P, NT * D])
        xnT = xs_raw[:, :].bitcast(F16).rearrange("p (c q n) -> p c q n", c=CH, q=2 * KD)
        s_all = xs_raw[:, :].rearrange("p (t d) -> p t d", d=D)
        WORK = 5 * KD * S + PIECES * PIECE
        work = sb("work", [P, WORK])
        at = [0]

        def part(raw, words):
            at[0] += words
            return raw[:, at[0] - words:at[0]]

        states = part(work, KD * S).rearrange("p (m n) -> p m n", m=KD)
        z = part(work, KD * S).rearrange("p (j d) -> p j d", d=D)
        gate = part(work, KD * S).rearrange("p (m n) -> p m n", m=KD)
        w = part(work, KD * S).rearrange("p (m n) -> p m n", m=KD)
        p_hi = part(work, KD * S // 2).bitcast(F16).rearrange("p (m n) -> p m n", m=KD)
        p_lo = part(work, KD * S // 2).bitcast(F16).rearrange("p (m n) -> p m n", m=KD)
        wst = part(work, PIECES * PIECE).rearrange("p (s n) -> p s n", s=PIECES)
        assert at[0] == WORK
        X_EARLY = PIECES * PIECE // D
        x_early = work[:, WORK - PIECES * PIECE:].rearrange("p (t d) -> p t d", d=D)
        wat_st = work[:, 0:4 * KD * D].rearrange("p (a k d) -> p a k d", a=4, k=KD)

        at[0] = 0
        slot_in = [part(rows_raw, SB * ROW // 2) for _ in range(2)]
        slot16 = [a.bitcast(F16).rearrange("p (s r) -> p s r", r=ROW) for a in slot_in]
        slot_words = [a.bitcast(I32).rearrange("p (s r) -> p s r", r=ROW // 2) for a in slot_in]
        slot32 = [a.rearrange("p (s r) -> p s r", r=ROW // 2) for a in slot_in]
        xT = [part(rows_raw, KD * BLOCK).bitcast(F16).rearrange("p (q n) -> p q n", q=2 * KD)
              for _ in range(2)]
        sil = [part(rows_raw, 2 * BLOCK).rearrange("p (m n) -> p m n", m=2) for _ in range(2)]
        g32 = [part(rows_raw, 2 * BLOCK).rearrange("p (m n) -> p m n", m=2) for _ in range(2)]
        g_hi = [part(rows_raw, KH * BLOCK // 2).bitcast(F16).rearrange("p (m n) -> p m n", m=KH)
                for _ in range(2)]
        g_lo = [part(rows_raw, KH * BLOCK // 2).bitcast(F16).rearrange("p (m n) -> p m n", m=KH)
                for _ in range(2)]
        ys = [part(rows_raw, SB * D).rearrange("p (s d) -> p s d", d=D) for _ in range(2)]
        half_bias = part(rows_raw, D)
        assert at[0] <= NT * ROW // 2

        at[0] = 0
        y_in = [part(w_raw, TPC * TOPK * D).rearrange("p (t c d) -> p t c d", t=TPC, c=TOPK)
                for _ in range(CH)]
        x_late = part(w_raw, (NT - PIECES * PIECE // D) * D).rearrange("p (t d) -> p t d", d=D)
        assert at[0] <= E * EW
        res = [a[:, :, 0, :] for a in y_in]

        at[0] = (E - 3) * EW // 2

        def routing(shape, dims, dt=F32, words=None):
            a = part(w_raw, (words or int(np.prod(shape))))
            a = a.bitcast(dt) if dt is not F32 else a
            return a.rearrange(f"p ({' '.join(dims)}) -> p {' '.join(dims)}", **dict(zip(dims, shape)))

        by_tile, by_expert = ((NT, E), "te"), ((E, NT), "et")
        e_of, lg_lo, lg, lg2, cand = [routing(*by_tile) for _ in range(5)]
        oh = [routing(*by_tile) for _ in range(TOPK)]
        seg, run, slot_of = [routing(*by_expert) for _ in range(3)]
        chosen = routing(*by_expert, dt=F16, words=E * NT // 2)
        blk_le = routing((BLOCKS, E), "be")
        pad_le = lg[:, 0:PADS, :]
        tok_row = routing((NT,), "t")
        blk_of = routing((BLOCKS,), "b")
        pad_no = routing((PADS,), "j")
        top, least, pos = [[routing((NT,), "t") for c in range(TOPK)] for _ in range(3)]
        th = routing((NT,), "t")
        pad_pos = routing((PADS,), "j")
        before = routing((P,), "k", dt=F16, words=P // 2)
        ones16 = routing((P,), "k", dt=F16, words=P // 2)
        n_blk_i = routing((E,), "e", dt=I32)
        n_blk, blk_end, blk_start, n_pads, pads_end = [routing((E,), "e") for _ in range(5)]
        assert at[0] <= E * EW // 2

        wat_hi = sb("wat_hi", [P, 4, KD, D], F16)
        wat_lo = sb("wat_lo", [P, 4, KD, D], F16)
        rt_st = sb("rt_st", [P, KD, E])
        rt = sb("rt", [P, KD, 2, E], F16)
        ident32 = sb("ident32", [P, P])
        ident16 = sb("ident16", [P, P], F16)
        fill32 = sb("fill32", [P, ROW // 2])
        cols = sb("cols", [P, 4, KD])
        neg_half = sb("neg_half", [P, TPC])
        spare = sb("spare", [P, 7])
        bn = [sb(f"bn{i}", [P, TPC, 6]) for i in range(2)]
        mv = [sb(f"mv{i}", [P, TPC, 2]) for i in range(2)]
        stat = [sb(f"stat{i}", [P, 3, TPC]) for i in range(2)]
        pad_pos_i = sb("pad_pos_i", [P, PADS], I32)
        blk_e = sb("blk_e", [P, BLOCKS])
        blk_off = sb("blk_off", [1, BLOCKS], I32)
        pos_i = [sb(f"pos_i{c}", [P, NT], I32) for c in range(TOPK)]
        is_first = [sb(f"is_first{i}", [P, SB]) for i in range(2)]
        gate_c = [sb(f"gate_c{i}", [P, SB]) for i in range(2)]
        dest_f = [sb(f"dest_f{i}", [P, SB]) for i in range(2)]
        dest = [sb(f"dest{i}", [P, SB], I32) for i in range(2)]

        bankA, bankB, bankC, bankD = [
            ctx.enter_context(nc.psum_tensor(f"bank{n}", [P, 2, 512], F32)) for n in "ABCD"]
        AB = [bankA, bankB]
        AB16 = [b[:, :, :].bitcast(F16) for b in AB]
        logits_ps = bankD[:, 0, :].rearrange("p (t h e) -> p t h e", t=NT, h=2)
        rank_ps = bankD[:, 1, 0:E * NT].rearrange("p (e t) -> p e t", e=E)
        total_ps = bankD[:, 1, E * NT:2 * E * NT].rearrange("p (e t) -> p e t", e=E)
        D16 = [bankD[:, i, :].bitcast(F16).rearrange("p (q n) -> p q n", q=2 * KD)
               for i in range(2)]

        x_loaded = [sem(f"x_loaded{i}") for i in range(2)]
        rt_loaded, wat_loaded, cols_loaded, bias_loaded = map(
            sem, ("rt_loaded", "wat_loaded", "cols_loaded", "bias_loaded"))
        wst_loaded = [sem(f"wst_loaded{i}") for i in range(PIECES)]
        consts, pool_step = sem("consts"), sem("pool_step")
        rt_hi, rt_split = sem("rt_hi"), sem("rt_split")
        lam_th, lam_ready, bias_halved = sem("lam_th"), sem("lam_ready"), sem("bias_halved")
        wat_hi_ready, wat_lo_ready = sem("wat_hi_ready"), sem("wat_lo_ready")
        bn_done, x_var, x_rstd, x_norm, x_hi, x_lo = map(
            sem, ("bn_done", "x_var", "x_rstd", "x_norm", "x_hi", "x_lo"))
        xt_hi_ps, xt_lo_ps, xt_hi_sb, xt_lo_sb = map(
            sem, ("xt_hi_ps", "xt_lo_ps", "xt_hi_sb", "xt_lo_sb"))
        logits_done, lg_lo_ready, route_step, chosen_ready, ranks_done = map(
            sem, ("logits_done", "lg_lo_ready", "route_step", "chosen_ready", "ranks_done"))
        tops_ready, th_ready, routed = map(sem, ("tops_ready", "th_ready", "routed"))
        pads_ready, rows_scattered = sem("pads_ready"), sem("rows_scattered")
        v_ps, q_ps, g_ps, yt_ps, zt_ps, o_ps = map(
            sem, ("v_ps", "q_ps", "g_ps", "yt_ps", "zt_ps", "o_ps"))
        states_ready, prod_ready, ybn_done, y_var, y_rstd, z_ready = map(
            sem, ("states_ready", "prod_ready", "ybn_done", "y_var", "y_rstd", "z_ready"))
        w_ready, gate_ready, p_ready, p_hi_ready, p_lo_ready, s_ready = map(
            sem, ("w_ready", "gate_ready", "p_ready", "p_hi_ready", "p_lo_ready", "s_ready"))
        w_hi_ready, w_lo_ready = sem("w_hi_ready"), sem("w_lo_ready")
        x_early_loaded, x_late_loaded = sem("x_early_loaded"), sem("x_late_loaded")
        slot_loaded = [sem(f"slot_loaded{i}") for i in range(2)]
        slot_t_ps, slot_t_sb, h_ps, sil_ready, g_ready, g_hi_ready, g_split, y_ps, y_sb = map(
            sem, ("slot_t_ps", "slot_t_sb", "h_ps", "sil_ready", "g_ready", "g_hi_ready",
                  "g_split", "y_ps", "y_sb"))
        meta_ready = sem("meta_ready")
        y_scattered = [sem(f"y_scattered{i}") for i in range(2)]
        y_loaded = [sem(f"y_loaded{c}") for c in range(CH)]
        moe_sum, moe_silu, gated, res_ready, late_ready = map(
            sem, ("moe_sum", "moe_silu", "gated", "res_ready", "late_ready"))
        stored = sem("stored")

        x_v = x.rearrange("(t p) d -> p t d", p=P)
        out_v = out.rearrange("(t p) d -> p t d", p=P)
        y_v = y_dram.rearrange("(t p c) d -> p t c d", p=P, c=TOPK)
        slots_v = slots_dram.rearrange("(n p) r -> p n r", p=P)
        w_exp_v = w_exp.rearrange("p (n w) -> p n w", w=PIECE)

        block = ctx.enter_context(nc.Block())

        @block.sync
        def _(sp):
            def load_x(g):
                for i in range(2):
                    if not isinstance(g, int) or g >= 2:
                        sp.wait_ge(x_loaded[i], g * 8)
                    sp.dma_start(xst[:, bass.ds(g * TPC + i * TPC, TPC), :],
                                 x_v[:, bass.ds(g * TPC + i * TPC, TPC), :]).then_inc(x_loaded[i], 16)
            repeat(sp, 2, CH, 2, load_x)

            def load_w(c):
                for i in range(PIECES):
                    if not isinstance(c, int):
                        sp.wait_ge(w_lo_ready, c * PIECES + (i + 1 - PIECES))
                    sp.dma_start(wst[:, i, :], w_exp_v[:, bass.ds(c * PIECES + i, 1), :].rearrange(
                        "p a w -> p (a w)")).then_inc(wst_loaded[i], 16)
            repeat(sp, 1, CONVERT, 1, load_w)

            sp.wait_ge(w_lo_ready, CONVERT * PIECES)
            sp.dma_start(x_early, x_v[:, 0:X_EARLY, :]).then_inc(x_early_loaded, 16)
            sp.wait_ge(rows_scattered, 16 * N_SCATTERS)

            def load_slots(b, i):
                if not isinstance(b, int) or b >= 2:
                    sp.wait_ge(slot_t_ps, b - 1)
                    sp.wait_ge(meta_ready, b - 1)
                sp.dma_start(slot_words[i], slots_v[:, bass.ds(b * SB, SB), :]).then_inc(slot_loaded[i], 16)

            def two(b):
                load_slots(b, 0)
                load_slots(b + 1, 1)
            repeat(sp, 2, BLOCKS - 1, 2, two)
            load_slots(BLOCKS - 1, (BLOCKS - 1) % 2)

            sp.wait_ge(y_scattered[0], 16 * SB * ((BLOCKS + 1) // 2))
            sp.wait_ge(y_scattered[1], 16 * SB * (BLOCKS // 2))

            for c in range(CH):
                sp.dma_start(y_in[c], y_v[:, c * TPC:(c + 1) * TPC, :, :]).then_inc(y_loaded[c], 16)
                if c == X_EARLY // TPC - 1:
                    sp.dma_start(x_late, x_v[:, X_EARLY:, :]).then_inc(x_late_loaded, 16)
            for c in range(CH):
                if c < X_EARLY // TPC:
                    sp.wait_ge(res_ready, c + 1)
                else:
                    sp.wait_ge(late_ready, c + 1 - X_EARLY // TPC)
                sp.dma_start(out_v[:, c * TPC:(c + 1) * TPC, :], res[c]).then_inc(stored, 16)
            sp.wait_ge(stored, 16 * CH)

        @block.gpsimd
        def _(pool):
            n = [0]

            def step(ins):
                n[0] += 1
                ins.then_inc(pool_step, 1)
                pool.wait_ge(pool_step, n[0])

            step(pool.memset(fill32[:, :], 0.0))
            step(pool.memset(fill32[:, D + META - 1:D + META], NO_ROW))
            pool.nop().then_inc(consts, 1)
            pool.memset(neg_half[:, :], -0.5)
            pool.memset(spare[:, :], 0.0)
            pool.memset(ident32[:, :], 0.0)
            pool.memset(before[:, :], 1.0)
            pool.memset(ones16[:, :], 1.0)
            step(pool.memset(ident16[:, :], 0.0))
            for m in (ident32, ident16):
                pool.affine_select(out=m[:, :], in_=m[:, :], compare_op=ALU.not_equal, fill=1.0,
                                   base=0, pattern=[[-1, P]], channel_multiplier=1)
            step(pool.affine_select(out=before[:, :], in_=before[:, :], compare_op=ALU.is_gt, fill=0.0,
                                    base=0, pattern=[[1, P]], channel_multiplier=-1))
            pool.nop().then_inc(consts, 1)

            def rstd(i, var_ready, count, out_ready):
                pool.wait_ge(var_ready, count)
                pool.tensor_scalar(stat[i][:, 2, :], mv[i][:, :, 0], -1.0, None, ALU.mult)
                step(pool.tensor_scalar(stat[i][:, 0, :], mv[i][:, :, 1], EPS, None, ALU.add))
                step(pool.tensor_tensor(stat[i][:, 1, :], stat[i][:, 0, :], neg_half[:, :], ALU.pow))
                pool.tensor_tensor(stat[i][:, 2, :], stat[i][:, 2, :], stat[i][:, 1, :],
                                   ALU.mult).then_inc(out_ready, 1)

            rstd(0, x_var, 1, x_rstd)
            rstd(1, x_var, 2, x_rstd)
            pool.iota(e_of[:, :, :], [[0, NT], [1, E]], base=0, channel_multiplier=0,
                      allow_small_or_imprecise_dtypes=True)
            pool.iota(tok_row[:, :], [[2 * P, NT]], base=1, channel_multiplier=2,
                      allow_small_or_imprecise_dtypes=True)
            pool.iota(blk_of[:, :], [[1, BLOCKS]], base=0, channel_multiplier=0,
                      allow_small_or_imprecise_dtypes=True)
            pool.iota(pad_no[:, :], [[P, PADS]], base=0, channel_multiplier=1,
                      allow_small_or_imprecise_dtypes=True)
            step(pool.memset(seg[:, :, :], 1.0))
            step(pool.memset(seg[:, :, 0:1], 0.0))
            pool.nop().then_inc(consts, 1)
            for g in range(2, CH):
                pool.wait_ge(x_norm, g - 1)
                rstd(g % 2, x_var, g + 1, x_rstd)

            scatters = [(pos_i[k][:, t:t + 1], row_words[:, t, :]) for t in range(NT) for k in range(TOPK)]
            scatters += [(pad_pos_i[:, j:j + 1], fill32[:, :].bitcast(I32)) for j in range(PADS)]
            per_chunk = N_SCATTERS // EARLY
            for c in range(EARLY):
                if c >= 1:
                    pool.wait_ge(z_ready, c)
                rstd(0, y_var, c + 1, y_rstd)
                if c == 0:
                    pool.wait_ge(routed, 1)
                if c == EARLY - 1:
                    pool.wait_ge(pads_ready, 1)
                for slot, row in scatters[c * per_chunk:(c + 1) * per_chunk if c < EARLY - 1 else None]:
                    pool.indirect_dma_start(
                        out=slots_dram, out_offset=bass.IndirectOffsetOnAxis(slot, 0),
                        in_=row, in_offset=None,
                        bounds_check=SLOTS - 1, oob_is_err=False).then_inc(rows_scattered, 16)

            n_meta = n[0]

            def meta(b, i, first):
                pool.wait_ge(slot_loaded[i], b * 8 + 16 if i == 0 else b * 8 + 8)
                if not first:
                    pool.wait_ge(y_sb, b - 1)
                    pool.wait_ge(y_scattered[i], b * 16 if i == 0 else b * 16 - 16)
                e_b = blk_e[:, bass.ds(b, 1)].to_broadcast([P, SB])
                pool.tensor_tensor(is_first[i][:, :], slot32[i][:, :, D], e_b, ALU.subtract)\
                    .then_inc(pool_step, 1)
                pool.wait_ge(pool_step, b * 3 + n_meta + 1)
                pool.tensor_tensor(spare[:, i:i + 1], spare[:, 6:7], spare[:, 6:7], ALU.add)
                pool.tensor_scalar(is_first[i][:, :], is_first[i][:, :], 0.0, None, ALU.is_equal)\
                    .then_inc(pool_step, 1)
                pool.wait_ge(pool_step, b * 3 + n_meta + 2)
                pool.tensor_tensor(gate_c[i][:, :], slot32[i][:, :, D + 1], is_first[i][:, :], ALU.mult)
                pool.tensor_tensor(dest_f[i][:, :], slot32[i][:, :, D + 3], is_first[i][:, :], ALU.subtract)\
                    .then_inc(pool_step, 1)
                pool.wait_ge(pool_step, b * 3 + n_meta + 3)
                pool.tensor_tensor(gate_c[i][:, :], gate_c[i][:, :], slot32[i][:, :, D + 2], ALU.add)
                pool.tensor_copy(dest[i][:, :], dest_f[i][:, :]).then_inc(meta_ready, 1)

            def scatter_y(b, i):
                pool.wait_ge(y_sb, b + 1)
                pool.wait_ge(meta_ready, b + 1)
                pool.tensor_tensor(spare[:, 2 + i:3 + i], spare[:, 6:7], spare[:, 6:7], ALU.add)
                for s in range(SB):
                    pool.indirect_dma_start(
                        out=y_dram, out_offset=bass.IndirectOffsetOnAxis(dest[i][:, s:s + 1], 0),
                        in_=ys[i][:, s, :], in_offset=None,
                        bounds_check=ROWS_OUT - 1, oob_is_err=False).then_inc(y_scattered[i], 16)

            pool.wait_ge(rows_scattered, 16 * N_SCATTERS)
            meta(0, 0, True)
            meta(1, 1, True)
            scatter_y(0, 0)
            with pool.Fori(2, BLOCKS - 2, 2) as b:
                meta(b, 0, False)
                scatter_y(b - 1, 1)
                meta(b + 1, 1, False)
                scatter_y(b, 0)
            meta(BLOCKS - 1, 0, False)
            scatter_y(BLOCKS - 2, 1)
            scatter_y(BLOCKS - 1, 0)

            n[0] += 3 * BLOCKS
            rstd(0, y_var, CH, y_rstd)
            pool.wait_ge(x_early_loaded, 16)
            for c in range(X_EARLY // TPC):
                pool.wait_ge(gated, c + 1)
                pool.tensor_tensor(res[c], res[c], x_early[:, c * TPC:(c + 1) * TPC, :], ALU.add)\
                    .then_inc(res_ready, 1)

        @block.scalar
        def _(act):
            act.dma_start(rt_st[:, :, :], router).then_inc(rt_loaded, 16)
            for n, a in enumerate((wq, wv, wg, wo)):
                act.dma_start(wat_st[:, n, :, :], a.rearrange("(k p) d -> p k d", p=P))\
                   .then_inc(wat_loaded, 16)
            for n, a in enumerate((beta, ln_g, ln_b)):
                act.dma_start(cols[:, n, :], a).then_inc(cols_loaded, 16)
            act.wait_ge(rt_loaded, 16)
            act.activation(rt[:, :, 0, :], rt_st[:, :, :], ACT.Copy, scale=WSCALE).then_inc(rt_hi, 1)
            act.wait_ge(cols_loaded, 48)
            act.activation(cols[:, 3, :], cols[:, 0, :], ACT.Tanh, scale=0.5).then_inc(lam_th, 1)

            act.wait_ge(wat_loaded, 64)
            act.activation(wat_hi[:, :, :, :], wat_st, ACT.Copy, scale=WSCALE).then_inc(wat_hi_ready, 1)

            def norm_x(g, i):
                act.wait_ge(x_rstd, g + 1)
                for j in range(TPC):
                    xt = xst[:, bass.ds(g * TPC + j, 1), :].rearrange("p a d -> p (a d)")
                    last = act.activation(xt, xt, ACT.Identity, bias=stat[i][:, 2, j:j + 1],
                                          scale=stat[i][:, 1, j:j + 1])
                last.then_inc(x_norm, 1)
                act.wait_ge(x_norm, g + 1)
                act.activation(rows16[:, bass.ds(g * TPC, TPC), 0:D], xst[:, bass.ds(g * TPC, TPC), :],
                               ACT.Copy).then_inc(x_hi, 1)

            def copy_xt_lo(g, i):
                act.wait_ge(xt_lo_ps, g + 1)
                act.activation(xnT[:, bass.ds(g, 1), KD:2 * KD, :].rearrange("p a q n -> p (a q n)"),
                               AB16[i][:, 1, :], ACT.Copy).then_inc(xt_lo_sb, 1)

            norm_x(0, 0)
            norm_x(1, 1)
            copy_xt_lo(0, 0)
            with act.Fori(2, CH - 1, 2) as g:
                norm_x(g, 0)
                copy_xt_lo(g - 1, 1)
                norm_x(g + 1, 1)
                copy_xt_lo(g, 0)
            copy_xt_lo(CH - 1, 1)

            act.wait_ge(logits_done, 1)
            act.activation(lg_lo[:, :, :], logits_ps[:, :, 1, :], ACT.Copy).then_inc(lg_lo_ready, 1)
            act.wait_ge(tops_ready, 1)
            act.activation(th[:, :], th[:, :], ACT.Tanh, scale=0.5 / WSCALE).then_inc(th_ready, 1)

            def affine(c):
                act.wait_ge(zt_ps, c)
                if not isinstance(c, int) or c >= 2:
                    act.wait_ge(p_lo_ready, KD * (c - 1))
                for m in range(KD):
                    act.activation(w[:, m, :], bankD[:, m, :], ACT.Identity, bias=cols[:, 2, m:m + 1],
                                   scale=cols[:, 1, m:m + 1]).then_inc(w_ready, 1)

            def split_p(c):
                if not isinstance(c, int) or c >= 2:
                    act.wait_ge(o_ps, c - 1)
                for m in range(KD):
                    act.wait_ge(p_ready, KD * (c - 1) + m + 1)
                    act.activation(p_hi[:, m, :], w[:, m, :], ACT.Copy).then_inc(p_hi_ready, 1)

            def keep_s(c):
                act.wait_ge(o_ps, c)
                act.activation(s_all[:, bass.ds(c * TPC - TPC, TPC), :].rearrange("p t d -> p (t d)"),
                               bankC[:, :, :].rearrange("p a b -> p (a b)"), ACT.Copy,
                               scale=1.0 / WSCALE).then_inc(s_ready, 1)

            def recur(c, convert=True):
                later = not isinstance(c, int) or c >= 1
                if later:
                    affine(c)
                    split_p(c)
                act.wait_ge(g_ps, c + 1)
                if later:
                    act.wait_ge(p_ready, KD * c)
                act.activation(gate, bankC[:, :, :], ACT.Silu, scale=1.0 / WSCALE).then_inc(gate_ready, 1)
                for i in range(PIECES if convert else 0):
                    act.wait_ge(wst_loaded[i], c * 16 + 16)
                    act.activation(w_hi[:, bass.ds((c * PIECES + i) * PIECE, PIECE)], wst[:, i, :],
                                   ACT.Copy, scale=WSCALE).then_inc(w_hi_ready, 1)
                act.wait_ge(y_rstd, c + 1)
                if later:
                    act.wait_ge(zt_ps, c)
                for j in range(TPC):
                    last = act.activation(z[:, j, :], bankD[:, j // 2, j % 2 * D:j % 2 * D + D],
                                          ACT.Identity, bias=stat[0][:, 2, j:j + 1],
                                          scale=stat[0][:, 1, j:j + 1])
                last.then_inc(z_ready, 1)
                if later:
                    keep_s(c)

            repeat(act, 1, CONVERT, 1, recur)
            for c in range(CONVERT, EARLY):
                recur(c, convert=False)

            def halves(b, i, first):
                for j in range(2):
                    act.wait_ge(h_ps, b * 2 + j + 1)
                    if first < 1:
                        act.wait_ge(g_ready, b * 2 - 1 + j)
                    act.activation(sil[j], AB[j][:, :, 0:BLOCK], ACT.Silu,
                                   scale=1.0 / WSCALE).then_inc(sil_ready, 1)
                    act.wait_ge(g_ready, b * 2 + j + 1)
                    if first < 0:
                        act.wait_ge(y_ps, b - 1)
                    act.activation(g_hi[i][:, 2 * j:2 * j + 2, :], g32[j], ACT.Copy)\
                       .then_inc(g_hi_ready, 1)

            act.wait_ge(rows_scattered, 16 * N_SCATTERS)
            act.dma_start(half_bias, bias).then_inc(bias_loaded, 16)
            halves(0, 0, 1)
            act.wait_ge(bias_loaded, 16)
            act.activation(half_bias, half_bias, ACT.Copy, scale=0.5).then_inc(bias_halved, 1)
            halves(1, 1, 0)
            with act.Fori(2, BLOCKS - 2, 2) as b:
                halves(b, 0, -1)
                halves(b + 1, 1, -1)
            halves(BLOCKS - 1, 0, -1)

            recur(EARLY, convert=False)
            for c in range(CH):
                if c == 3:
                    affine(CH)
                    split_p(CH)
                if c == 5:
                    keep_s(CH)
                act.wait_ge(moe_sum, c + 1)
                act.activation(res[c], res[c], ACT.Silu).then_inc(moe_silu, 1)

        @block.vector
        def _(dve):
            n = [0]

            def step(ins):
                n[0] += 1
                ins.then_inc(route_step, 1)
                dve.wait_ge(route_step, n[0])

            dve.wait_ge(rt_hi, 1)
            dve.scalar_tensor_tensor(rt[:, :, 1, :], rt_st[:, :, :], WSCALE, rt[:, :, 0, :],
                                     ALU.mult, ALU.subtract).then_inc(rt_split, 1)

            dve.wait_ge(lam_th, 1)
            dve.tensor_scalar(cols[:, 3, :], cols[:, 3, :], 0.5, 0.5, ALU.mult, ALU.add)\
               .then_inc(lam_ready, 1)

            def stats_x(g, i):
                dve.wait_ge(x_loaded[i], (g * 8 + 16) if i == 0 else (g * 8 + 8))
                later = not isinstance(g, int) or g >= 2
                if later:
                    dve.wait_ge(x_var, g - 1)
                for j in range(TPC):
                    last = dve.bn_stats(bn[i][:, j, :],
                                        xst[:, bass.ds(g * TPC + j, 1), :].rearrange("p a d -> p (a d)"))
                last.then_inc(bn_done, 1)
                dve.wait_ge(bn_done, g + 1)
                if later:
                    dve.wait_ge(x_rstd, g - 1)
                dve.memset(spare[:, 4 + i:5 + i], 0.0)
                for j in range(TPC):
                    last = dve.bn_aggr(mv[i][:, j, :], bn[i][:, j, :])
                last.then_inc(x_var, 1)

            def split_x(g, i, more=True):
                dve.wait_ge(x_hi, g + 1)
                tiles = bass.ds(g * TPC, TPC)
                dve.tensor_tensor(rows16[:, tiles, D:2 * D], xst[:, tiles, :], rows16[:, tiles, 0:D],
                                  ALU.subtract).then_inc(x_lo, 1)
                if more:
                    stats_x(g + 2, i)
                dve.wait_ge(xt_hi_ps, g + 1)
                dve.tensor_copy(xnT[:, bass.ds(g, 1), 0:KD, :].rearrange("p a q n -> p (a q n)"),
                                AB16[i][:, 0, :]).then_inc(xt_hi_sb, 1)

            dve.wait_ge(consts, 2)
            stats_x(0, 0)
            stats_x(1, 1)
            dve.wait_ge(wat_hi_ready, 1)
            dve.scalar_tensor_tensor(wat_lo[:, :, :, :], wat_st, WSCALE, wat_hi[:, :, :, :],
                                     ALU.mult, ALU.subtract).then_inc(wat_lo_ready, 1)
            with dve.Fori(0, CH - 3, 2) as g:
                split_x(g, 0)
                split_x(g + 1, 1)
            split_x(CH - 2, 0, False)
            split_x(CH - 1, 1, False)

            def tiles_of(a):
                return a[:, :].unsqueeze(2).to_broadcast([P, NT, E])

            dve.wait_ge(lg_lo_ready, 1)
            dve.wait_ge(consts, 3)
            step(dve.tensor_tensor(lg[:, :, :], logits_ps[:, :, 0, :], lg_lo[:, :, :], ALU.add))
            src = lg
            for c in range(TOPK):
                step(dve.tensor_reduce(top[c][:, :], src[:, :, :], AX.X, ALU.max))
                step(dve.tensor_tensor(cand[:, :, :], src[:, :, :], tiles_of(top[c]), ALU.is_equal))
                step(dve.scalar_tensor_tensor(cand[:, :, :], cand[:, :, :], -16.0, e_of[:, :, :],
                                              ALU.mult, ALU.add))
                step(dve.tensor_reduce(least[c][:, :], cand[:, :, :], AX.X, ALU.min))
                step(dve.tensor_tensor(oh[c][:, :, :], cand[:, :, :], tiles_of(least[c]), ALU.is_equal))
                if c == 0:
                    step(dve.scalar_tensor_tensor(lg2[:, :, :], oh[0][:, :, :], MASKED, lg[:, :, :],
                                                  ALU.mult, ALU.add))
                    src = lg2
            dve.tensor_tensor(chosen[:, :, :].rearrange("p e t -> p t e"), oh[0][:, :, :], oh[1][:, :, :],
                              ALU.add).then_inc(chosen_ready, 1)
            dve.tensor_tensor(th[:, :], top[0][:, :], top[1][:, :], ALU.subtract).then_inc(tops_ready, 1)

            dve.wait_ge(ranks_done, 1)
            flat = "p e t -> p (e t)"
            step(dve.tensor_tensor_scan(run[:, :, :].rearrange(flat), seg[:, :, :].rearrange(flat),
                                        total_ps.rearrange(flat), 0.0, ALU.mult, ALU.add))
            n_e = run[:, :, NT - 1]
            step(dve.tensor_scalar(n_blk_i[:, :], n_e, float(BLOCK - 1), None, ALU.add))
            step(dve.tensor_single_scalar(n_blk_i[:, :], n_blk_i[:, :], BLOCK.bit_length() - 1,
                                          ALU.logical_shift_right))
            step(dve.tensor_copy(n_blk[:, :], n_blk_i[:, :]))
            step(dve.tensor_tensor_scan(blk_end[:, :], seg[:, 0, 1:E + 1], n_blk[:, :], 0.0,
                                        ALU.mult, ALU.add))
            step(dve.tensor_tensor(blk_start[:, :], blk_end[:, :], n_blk[:, :], ALU.subtract))
            step(dve.tensor_tensor(slot_of[:, :, :], run[:, :, :], total_ps, ALU.subtract))
            step(dve.tensor_tensor(slot_of[:, :, :], slot_of[:, :, :], rank_ps, ALU.add))
            step(dve.scalar_tensor_tensor(slot_of[:, :, :],
                                          blk_start[:, :].unsqueeze(2).to_broadcast([P, E, NT]),
                                          float(BLOCK), slot_of[:, :, :], ALU.mult, ALU.add))
            for c in range(TOPK):
                step(dve.tensor_tensor(cand[:, :, :], oh[c][:, :, :],
                                       slot_of[:, :, :].rearrange("p e t -> p t e"), ALU.mult))
                step(dve.tensor_reduce(pos[c][:, :], cand[:, :, :], AX.X, ALU.add))
                dve.tensor_copy(pos_i[c][:, :], pos[c][:, :])
            dve.tensor_copy(rows32[:, :, D], least[0][:, :])
            dve.tensor_copy(rows32[:, :, D + 3], tok_row[:, :])
            dve.wait_ge(th_ready, 1)
            dve.tensor_scalar(rows32[:, :, D + 1], th[:, :], 1.0 / WSCALE, None, ALU.mult)
            dve.tensor_scalar(rows32[:, :, D + 2], th[:, :], -0.5 / WSCALE, 0.5 / WSCALE, ALU.mult, ALU.add)\
               .then_inc(routed, 1)
            def route_blocks():
                step(dve.tensor_tensor(blk_le[:, :, :], blk_end[:, :].unsqueeze(1).to_broadcast([P, BLOCKS, E]),
                                       blk_of[:, :].unsqueeze(2).to_broadcast([P, BLOCKS, E]), ALU.is_le))
                step(dve.tensor_reduce(blk_e[:, :], blk_le[:, :, :], AX.X, ALU.add))
                step(dve.tensor_single_scalar(blk_e[:, :], blk_e[:, :], float(E - 1), ALU.min))
                step(dve.tensor_single_scalar(blk_off[:, :], blk_e[0:1, :], float(EW), ALU.mult))
                step(dve.tensor_single_scalar(blk_e[:, :], blk_e[:, :], -16.0, ALU.add))
                n_e_bc = n_e.unsqueeze(1).to_broadcast([P, PADS, E])
                step(dve.scalar_tensor_tensor(n_pads[:, :], n_blk[:, :], float(BLOCK), n_e, ALU.mult, ALU.subtract))
                step(dve.tensor_tensor_scan(pads_end[:, :], seg[:, 0, 1:E + 1], n_pads[:, :], 0.0,
                                            ALU.mult, ALU.add))
                step(dve.tensor_tensor(pads_end[:, :], pads_end[:, :], n_pads[:, :], ALU.subtract))
                step(dve.tensor_tensor(pad_le[:, :, :], pads_end[:, :].unsqueeze(1).to_broadcast([P, PADS, E]),
                                       pad_no[:, :].unsqueeze(2).to_broadcast([P, PADS, E]), ALU.is_le))
                step(dve.tensor_tensor(pad_le[:, :, :], pad_le[:, :, :], n_e_bc, ALU.mult))
                step(dve.tensor_reduce(pad_pos[:, :], pad_le[:, :, :], AX.X, ALU.add))
                dve.tensor_tensor(pad_pos_i[:, :], pad_pos[:, :], pad_no[:, :], ALU.add).then_inc(pads_ready, 1)

            dve.wait_ge(lam_ready, 1)

            def recur(c, convert=True):
                later = not isinstance(c, int) or c >= 1
                dve.wait_ge(v_ps, c + 1)
                if later:
                    dve.wait_ge(yt_ps, c)
                for m in range(KD):
                    last = dve.tensor_tensor_scan(states[:, m, :], cols[:, 3, m:m + 1].to_broadcast([P, S]),
                                                  bankA[:, m, :], 0.0, ALU.mult, ALU.add)
                last.then_inc(states_ready, 1)
                dve.wait_ge(q_ps, c + 1)
                dve.wait_ge(states_ready, c + 1)
                dve.scalar_tensor_tensor(states, bankB[:, :, :], 1.0 / WSCALE ** 2, states, ALU.mult, ALU.mult)\
                   .then_inc(prod_ready, 1)
                if later:
                    times_gate(c)
                else:
                    route_blocks()
                dve.wait_ge(yt_ps, c + 1)
                if later:
                    dve.wait_ge(y_var, c)
                else:
                    dve.wait_ge(x_var, CH)
                for j in range(TPC):
                    last = dve.bn_stats(bn[0][:, j, :], bankD[:, j // 2, j % 2 * D:j % 2 * D + D])
                last.then_inc(ybn_done, 1)
                dve.wait_ge(ybn_done, c + 1)
                if later:
                    dve.wait_ge(y_rstd, c)
                dve.memset(spare[:, 4:5], 0.0)
                for j in range(TPC):
                    last = dve.bn_aggr(mv[0][:, j, :], bn[0][:, j, :])
                last.then_inc(y_var, 1)
                for i in range(PIECES if convert else 0):
                    dve.wait_ge(w_hi_ready, c * PIECES + (i + 1))
                    piece = bass.ds((c * PIECES + i) * PIECE, PIECE)
                    dve.scalar_tensor_tensor(w_lo[:, piece], wst[:, i, :], WSCALE, w_hi[:, piece],
                                             ALU.mult, ALU.subtract).then_inc(w_lo_ready, 1)

            def times_gate(c):
                for m in range(KD):
                    dve.wait_ge(w_ready, KD * (c - 1) + m + 1)
                    if m == 0:
                        dve.wait_ge(gate_ready, c)
                    dve.tensor_tensor(w[:, m, :], w[:, m, :], gate[:, m, :], ALU.mult).then_inc(p_ready, 1)
                for m in range(KD):
                    dve.wait_ge(p_hi_ready, KD * (c - 1) + m + 1)
                    dve.tensor_tensor(p_lo[:, m, :], w[:, m, :], p_hi[:, m, :], ALU.subtract)\
                       .then_inc(p_lo_ready, 1)

            repeat(dve, 1, CONVERT, 1, recur)
            for c in range(CONVERT, EARLY):
                recur(c, convert=False)

            dve.wait_ge(rows_scattered, 16 * N_SCATTERS)
            def copy_xt(b, i, first):
                dve.wait_ge(slot_t_ps, b + 1)
                if not first:
                    dve.wait_ge(h_ps, b * 2 - 2)
                dve.tensor_copy(xT[i], D16[i]).then_inc(slot_t_sb, 1)

            def half(b, i, j):
                dve.wait_ge(sil_ready, b * 2 + j + 1)
                dve.scalar_tensor_tensor(g32[j], sil[j], 1.0 / WSCALE, AB[j][:, :, BLOCK:2 * BLOCK],
                                         ALU.mult, ALU.mult).then_inc(g_ready, 1)
                dve.wait_ge(g_hi_ready, b * 2 + j + 1)
                dve.tensor_tensor(g_lo[i][:, 2 * j:2 * j + 2, :], g32[j], g_hi[i][:, 2 * j:2 * j + 2, :],
                                  ALU.subtract).then_inc(g_split, 1)

            def gate_y(b, i, first):
                dve.wait_ge(y_ps, b + 1)
                dve.wait_ge(meta_ready, b + 1)
                if not first:
                    dve.wait_ge(y_scattered[i], b * 16 if i == 0 else b * 16 - 16)
                for s in range(SB):
                    last = dve.scalar_tensor_tensor(ys[i][:, s, :], bankC[:, i, s * D:s * D + D],
                                                    gate_c[i][:, s:s + 1], half_bias,
                                                    ALU.mult, ALU.add)
                last.then_inc(y_sb, 1)

            def blocks(b, i, first, last=False):
                half(b, i, 0)
                if not last:
                    copy_xt(b + 1, 1 - i, first)
                half(b, i, 1)
            copy_xt(0, 0, True)
            blocks(0, 0, True)
            blocks(1, 1, False)
            dve.wait_ge(bias_halved, 1)
            gate_y(0, 0, True)
            with dve.Fori(2, BLOCKS - 2, 2) as b:
                blocks(b, 0, False)
                gate_y(b - 1, 1, False)
                blocks(b + 1, 1, False)
                gate_y(b, 0, False)
            blocks(BLOCKS - 1, 0, False, True)
            gate_y(BLOCKS - 2, 1, False)
            gate_y(BLOCKS - 1, 0, False)

            recur(EARLY, convert=False)

            def sum_y(c):
                dve.wait_ge(y_loaded[c], 16)
                dve.tensor_tensor(res[c], y_in[c][:, :, 0, :], y_in[c][:, :, 1, :], ALU.add)\
                   .then_inc(moe_sum, 1)

            for c in range(CH):
                if c == 0:
                    sum_y(0)
                if c == 2:
                    times_gate(CH)
                if c + 1 < CH:
                    sum_y(c + 1)
                dve.wait_ge(moe_silu, c + 1)
                dve.wait_ge(s_ready, c + 1)
                dve.tensor_tensor(res[c], res[c], s_all[:, c * TPC:(c + 1) * TPC, :], ALU.mult)\
                   .then_inc(gated, 1)
                if c >= X_EARLY // TPC:
                    dve.wait_ge(gated, c + 1)
                    dve.wait_ge(x_late_loaded, 16)
                    dve.tensor_tensor(res[c], res[c], x_late[:, c * TPC - X_EARLY:(c + 1) * TPC - X_EARLY, :],
                                      ALU.add).then_inc(late_ready, 1)

        @block.tensor
        def _(pe):
            def three(out_ap, pairs, hi_l, lo_l, hi_r, lo_r):
                todo = [(a(k), b(k)) for k in pairs for a, b in ((hi_l, hi_r), (hi_l, lo_r), (lo_l, hi_r))]
                for n, (lhsT, rhs) in enumerate(todo):
                    last = pe.matmul(out_ap, lhsT, rhs, start=(n == 0), stop=(n == len(todo) - 1))
                return last

            pe.wait_ge(consts, 2)

            def transpose_x(g, i):
                for h, (ready, done, free) in enumerate(((x_hi, xt_hi_ps, xt_hi_sb),
                                                         (x_lo, xt_lo_ps, xt_lo_sb))):
                    pe.wait_ge(ready, g + 1)
                    if not isinstance(g, int) or g >= 2:
                        pe.wait_ge(free, g - 1)
                    for j in range(TPC):
                        for k in range(KD):
                            src = rows16[:, bass.ds(g * TPC + j, 1), h * D + k * P:h * D + k * P + P]
                            last = pe.transpose(AB16[i][:, h, k * S + j * P:k * S + j * P + P],
                                                src.rearrange("p a d -> p (a d)"), ident16[:, :])
                    last.then_inc(done, 1)

            def route_x(g):
                pe.wait_ge(xt_hi_sb, g + 1)
                pe.wait_ge(xt_lo_sb, g + 1)
                for j in range(TPC):
                    dst = logits_ps[:, bass.ds(g * TPC + j, 1), :, :].rearrange("p a h e -> p (a h e)")
                    for q in range(2 * KD):
                        last = pe.matmul(dst, xnT[:, bass.ds(g, 1), q, j * P:j * P + P].rearrange(
                            "p a n -> p (a n)"), rt[:, q % KD, :, :].rearrange("p h e -> p (h e)"),
                            start=(q == 0), stop=(q == 2 * KD - 1))
                return last

            transpose_x(0, 0)
            transpose_x(1, 1)
            pe.wait_ge(rt_split, 1)
            route_x(0)
            with pe.Fori(2, CH - 1, 2) as g:
                transpose_x(g, 0)
                route_x(g - 1)
                transpose_x(g + 1, 1)
                route_x(g)
            route_x(CH - 1).then_inc(logits_done, 1)

            def project(bank, a, c):
                for m in range(KD):
                    last = three(bank[:, m, :], range(KD),
                                 lambda k: wat_hi[:, a, k, m * P:m * P + P],
                                 lambda k: wat_lo[:, a, k, m * P:m * P + P],
                                 lambda k: xnT[:, bass.ds(c, 1), k, :].rearrange("p a n -> p (a n)"),
                                 lambda k: xnT[:, bass.ds(c, 1), KD + k, :].rearrange("p a n -> p (a n)"))
                return last

            def transpose_z(c, after_blocks=False):
                pe.wait_ge(z_ready, c)
                if after_blocks:
                    pe.wait_ge(slot_t_sb, BLOCKS)
                for j in range(TPC):
                    for m in range(KD):
                        last = pe.transpose(bankD[:, m, j * P:j * P + P], z[:, j, m * P:m * P + P],
                                            ident32[:, :])
                last.then_inc(zt_ps, 1)

            def project_out(c):
                pe.wait_ge(p_lo_ready, KD * c)
                for j in range(TPC):
                    last = three(bankC[:, j // 2, j % 2 * D:j % 2 * D + D], range(KD),
                                 lambda k: p_hi[:, k, j * P:j * P + P],
                                 lambda k: p_lo[:, k, j * P:j * P + P],
                                 lambda k: wat_hi[:, 3, k, :],
                                 lambda k: wat_lo[:, 3, k, :])
                last.then_inc(o_ps, 1)

            pe.wait_ge(wat_lo_ready, 1)

            def recur(c, after_blocks=False):
                later = not isinstance(c, int) or c >= 1
                if after_blocks:
                    pe.wait_ge(g_ready, 2 * BLOCKS)
                    pe.wait_ge(y_sb, BLOCKS)
                elif later:
                    pe.wait_ge(states_ready, c)
                project(bankA, 1, c).then_inc(v_ps, 1)
                if later:
                    pe.wait_ge(prod_ready, c)
                project(bankB, 0, c).then_inc(q_ps, 1)
                if later:
                    transpose_z(c, after_blocks)
                else:
                    pe.wait_ge(chosen_ready, 1)
                    chosen_v = chosen[:, :, :].rearrange("p e t -> p (e t)")
                    pe.matmul(rank_ps.rearrange("p e t -> p (e t)"), before[:, :], chosen_v,
                              start=True, stop=True)
                    pe.matmul(total_ps.rearrange("p e t -> p (e t)"), ones16[:, :], chosen_v,
                              start=True, stop=True).then_inc(ranks_done, 1)
                if not isinstance(c, int) or c >= 2:
                    pe.wait_ge(s_ready, c - 1)
                project(bankC, 2, c).then_inc(g_ps, 1)
                pe.wait_ge(prod_ready, c + 1)
                if later:
                    pe.wait_ge(w_ready, KD * c)
                for j in range(TPC):
                    for m in range(KD):
                        last = pe.transpose(bankD[:, j // 2, j % 2 * D + m * P:j % 2 * D + m * P + P],
                                            states[:, m, j * P:j * P + P], ident32[:, :])
                last.then_inc(yt_ps, 1)
                if later:
                    pe.wait_ge(gate_ready, c + 1)
                    project_out(c)
            repeat(pe, 1, EARLY, 1, recur)

            def weights_at(b):
                return pe.value_load(blk_off[0:1, bass.ds(b, 1)], min_val=0, max_val=(E - 1) * EW)

            def transpose_slots(b, i, first):
                pe.wait_ge(slot_loaded[i], b * 8 + 16 if i == 0 else b * 8 + 8)
                if not first:
                    pe.wait_ge(slot_t_sb, b - 1)
                for q in range(2 * KD):
                    for s in range(SB):
                        last = pe.transpose(D16[i][:, q, s * P:s * P + P],
                                            slot16[i][:, s, q * P:q * P + P], ident16[:, :])
                last.then_inc(slot_t_ps, 1)

            def hidden(b, i, j, off, first):
                if not first:
                    pe.wait_ge(g_ready, b * 2 - 1 + j)
                for m in (2 * j, 2 * j + 1):
                    for half in range(2):
                        col = half * HID + m * P
                        last = three(AB[j][:, m % 2, half * BLOCK:half * BLOCK + BLOCK], range(KD),
                                     lambda k: w_hi[:, bass.ds(off + (k * 2 * HID + col), P)],
                                     lambda k: w_lo[:, bass.ds(off + (k * 2 * HID + col), P)],
                                     lambda k: xT[i][:, k, :],
                                     lambda k: xT[i][:, KD + k, :])
                last.then_inc(h_ps, 1)

            def outputs(b, i, off, first):
                pe.wait_ge(g_split, b * 2 + 2)
                if not first:
                    pe.wait_ge(y_sb, b - 1)
                for s in range(SB):
                    last = three(bankC[:, i, s * D:s * D + D], range(KH),
                                 lambda k: g_hi[i][:, k, s * P:s * P + P],
                                 lambda k: g_lo[i][:, k, s * P:s * P + P],
                                 lambda k: w_hi[:, bass.ds(off + (KD * 2 * HID + k * D), D)],
                                 lambda k: w_lo[:, bass.ds(off + (KD * 2 * HID + k * D), D)])
                last.then_inc(y_ps, 1)

            def one_block(b, i, first=False, last=False, second=False, third=False):
                off = weights_at(b)
                pe.wait_ge(slot_t_sb, b + 1)
                hidden(b, i, 0, off, first)
                if not last:
                    transpose_slots(b + 1, 1 - i, first)
                hidden(b, i, 1, off, first)
                if not first:
                    outputs(b - 1, 1 - i, weights_at(b - 1), second or third)

            pe.wait_ge(w_lo_ready, CONVERT * PIECES)
            pe.wait_ge(z_ready, EARLY)
            pe.wait_ge(s_ready, EARLY - 1)
            transpose_slots(0, 0, True)
            one_block(0, 0, first=True)
            one_block(1, 1, second=True)
            with pe.Fori(2, BLOCKS - 2, 2) as b:
                one_block(b, 0)
                one_block(b + 1, 1)
            one_block(BLOCKS - 1, 0, last=True)
            outputs(BLOCKS - 1, 0, weights_at(BLOCKS - 1), False)

            recur(EARLY, True)
            transpose_z(CH)
            project_out(CH)


_OUT_SHAPE = (B, S, D)


def kernel(L0_attn_x, L0_attn_Wq, L0_attn_Wv, L0_attn_Wg, L0_attn_Wo, L0_attn_beta, L0_attn_ln_g,
           L0_attn_ln_b, L0_ffn_router_weight, L0_ffn_w_in, L0_ffn_w_out, L0_ffn_bias):
    import concourse.bacc as bacc
    from concourse.bass_utils import run_bass_kernel_spmd

    def by_partition(a):
        return np.ascontiguousarray(a.reshape(KD, P, -1).transpose(1, 0, 2))

    def column(a):
        return np.ascontiguousarray(a.reshape(KD, P).T)

    w_in = np.asarray(L0_ffn_w_in).reshape(E, 2 * HID, KD, P).transpose(3, 0, 2, 1)
    w_out = np.asarray(L0_ffn_w_out).reshape(E, D, KH, P).transpose(3, 0, 2, 1)
    w_exp = np.concatenate([w_in.reshape(P, E, -1), w_out.reshape(P, E, -1)], axis=2).reshape(P, E * EW)
    arrays = {
        "x": np.asarray(L0_attn_x).reshape(T, D),
        "wq": np.asarray(L0_attn_Wq), "wv": np.asarray(L0_attn_Wv),
        "wg": np.asarray(L0_attn_Wg), "wo": np.asarray(L0_attn_Wo),
        "beta": column(np.repeat(np.asarray(L0_attn_beta), D // NH)),
        "ln_g": column(np.asarray(L0_attn_ln_g)), "ln_b": column(np.asarray(L0_attn_ln_b)),
        "router": by_partition(np.asarray(L0_ffn_router_weight).T),
        "w_exp": w_exp,
        "bias": np.broadcast_to(np.asarray(L0_ffn_bias), (P, D)),
    }
    arrays = {f"{k}_in": np.ascontiguousarray(v) for k, v in arrays.items()}
    nc = bacc.Bacc("TRN2", target_bir_lowering=False, num_devices=1)
    args = [nc.dram_tensor(k, v.shape, mybir.dt.from_np(v.dtype), kind="ExternalInput").ap()
            for k, v in arrays.items()]
    out = nc.dram_tensor("out", (T, D), F32, kind="ExternalOutput").ap()
    build(nc, *args, out)
    r = run_bass_kernel_spmd(nc, [arrays], core_ids=[0])
    return r.results[0]["out"].reshape(_OUT_SHAPE)
```

```python
from contextlib import ExitStack

import numpy as np

import concourse.bass as bass
from concourse import mybir

F32, F16, I32 = mybir.dt.float32, mybir.dt.float16, mybir.dt.int32
ALU, ACT, AX = mybir.AluOpType, mybir.ActivationFunctionType, mybir.AxisListType

P = 128
B, S, D = 8, 512, 256
T = B * S
NT = T // P
KD = D // P
TPC = S // P
CH = B
NH = 16
E, HID, TOPK = 8, 512, 2
KH = HID // P
BLOCK = 256
SB = BLOCK // P
BLOCKS = (TOPK * T + E * (BLOCK - 1)) // BLOCK
REGION = T + BLOCK
SLOTS = E * REGION + BLOCK
META = 4
ROW = D + META
EW = KD * 2 * HID + KH * D
EARLY = CH - 2
PIECES = 4
PIECE = E * EW // (EARLY * PIECES)
STAGES = 4
X_EARLY = 7
AHEAD = 4
X_POOL = 6
SUMS_POOL = (1, 2, 3, 4)
GROUPS = 2
GT = NT // GROUPS
GC = CH // GROUPS
WSCALE = 16.0
EPS = 1e-5
MASKED = -3.0e38
ROWS_OUT = TOPK * T
NO_ROW = float(ROWS_OUT + 1)
N_SCATTERS = TOPK * NT
SCATTERS_FIRST = 14
SCATTERS_EACH = 11


def repeat(eng, peeled, end, stride, body):
    for i in range(0, peeled, stride):
        body(i)
    with eng.Fori(peeled, end - stride + 1, stride) as i:
        body(i)


def build(nc, x, wq, wv, wg, wo, beta, ln_g, ln_b, router, w_exp, bias, out):
    ctx = ExitStack()
    with ctx:
        def sb(name, shape, dt=F32):
            return ctx.enter_context(nc.sbuf_tensor(name, shape, dt))

        def sem(name):
            return ctx.enter_context(nc.semaphore(name))

        slots_dram = nc.dram_tensor("slots_dram", (SLOTS, ROW), F32).ap()
        y_dram = nc.dram_tensor("y_dram", (ROWS_OUT, D), F32).ap()

        w_raw = sb("w_raw", [P, E * EW])
        w_hi = w_raw[:, 0:E * EW // 2].bitcast(F16)
        w_lo = w_raw[:, E * EW // 2:E * EW].bitcast(F16)
        xst = w_raw[:, E * EW - NT * D:E * EW].rearrange("p (t d) -> p t d", d=D)
        rows_raw = sb("rows_raw", [P, NT * ROW])
        rows = rows_raw[:, :].rearrange("p (t r) -> p t r", r=ROW)
        xs_raw = sb("xs_raw", [P, NT * D])
        xnT = xs_raw[:, :].bitcast(F16).rearrange("p (c q n) -> p c q n", c=CH, q=2 * KD)
        s_all = xs_raw[:, :].rearrange("p (t d) -> p t d", d=D)
        WORK = 5 * KD * S + STAGES * PIECE
        work = sb("work", [P, WORK])
        at = [0]

        def part(raw, words):
            at[0] += words
            return raw[:, at[0] - words:at[0]]

        def recurrence_buffers(raw):
            n = KD * S
            return (part(raw, n).rearrange("p (m n) -> p m n", m=KD),
                    part(raw, n).rearrange("p (m n) -> p m n", m=KD),
                    part(raw, n // 2).bitcast(F16).rearrange("p (m n) -> p m n", m=KD),
                    part(raw, n // 2).bitcast(F16).rearrange("p (m n) -> p m n", m=KD))

        z = part(work, KD * S).rearrange("p (j d) -> p j d", d=D)
        gate = part(work, KD * S).rearrange("p (m n) -> p m n", m=KD)
        x_early = work[:, at[0]:WORK].rearrange("p (t d) -> p t d", d=D)
        early_buffers = recurrence_buffers(work)
        wst = part(work, STAGES * PIECE).rearrange("p (s n) -> p s n", s=STAGES)
        assert at[0] == WORK and X_EARLY * TPC * D == WORK - 2 * KD * S
        wat_st = work[:, 0:4 * KD * D].rearrange("p (a k d) -> p a k d", a=4, k=KD)

        at[0] = 0
        slot_in = [part(rows_raw, SB * ROW).rearrange("p (s r) -> p s r", r=ROW) for _ in range(2)]
        xT = [part(rows_raw, KD * BLOCK).bitcast(F16).rearrange("p (q n) -> p q n", q=2 * KD)
              for _ in range(2)]
        sil = [part(rows_raw, 2 * BLOCK).rearrange("p (m n) -> p m n", m=2) for _ in range(2)]
        g32 = [part(rows_raw, 2 * BLOCK).rearrange("p (m n) -> p m n", m=2) for _ in range(2)]
        g_hi = [part(rows_raw, KH * BLOCK // 2).bitcast(F16).rearrange("p (m n) -> p m n", m=KH)
                for _ in range(2)]
        g_lo = [part(rows_raw, KH * BLOCK // 2).bitcast(F16).rearrange("p (m n) -> p m n", m=KH)
                for _ in range(2)]
        ys = [part(rows_raw, SB * D).rearrange("p (s d) -> p s d", d=D) for _ in range(2)]
        half_bias = part(rows_raw, D)
        is_first, gate_c, dest_f = [[part(rows_raw, SB) for _ in range(2)] for _ in range(3)]
        dest = [part(rows_raw, SB).bitcast(I32) for _ in range(2)]
        assert at[0] <= NT * ROW

        at[0] = 0
        y_in = [part(w_raw, TPC * TOPK * D).rearrange("p (t c d) -> p t c d", t=TPC, c=TOPK)
                for _ in range(CH)]
        x_late = part(w_raw, (CH - X_EARLY) * TPC * D).rearrange("p (t d) -> p t d", d=D)
        late_buffers = recurrence_buffers(w_raw)
        assert at[0] <= E * EW
        res = [a[:, :, 0, :] for a in y_in]

        def x_of(c):
            return (x_early[:, c * TPC:(c + 1) * TPC, :] if c < X_EARLY else
                    x_late[:, (c - X_EARLY) * TPC:(c - X_EARLY + 1) * TPC, :])

        at[0] = (E - 3) * EW // 2

        def routing(shape, dims, dt=F32, words=None):
            a = part(w_raw, (words or int(np.prod(shape))))
            a = a.bitcast(dt) if dt is not F32 else a
            return a.rearrange(f"p ({' '.join(dims)}) -> p {' '.join(dims)}", **dict(zip(dims, shape)))

        by_tile, by_expert = ((NT, E), "te"), ((GROUPS, E, GT), "get")
        e_of, lg2, cand = [routing(*by_tile) for _ in range(3)]
        oh = [routing(*by_tile) for _ in range(TOPK)]
        run, slot_of = [routing(*by_expert) for _ in range(2)]
        seg = routing((E, GT), "et")
        chosen = routing(*by_expert, dt=F16, words=E * NT // 2)
        blk_le = routing((BLOCKS, E), "be")
        blk_n = routing((BLOCKS, E), "be")
        blk_s, blk_row_f, blk_e8 = [routing((BLOCKS,), "b") for _ in range(3)]
        tok_row = routing((NT,), "t")
        blk_of = routing((BLOCKS,), "b")
        top, least, pos = [[routing((NT,), "t") for c in range(TOPK)] for _ in range(3)]
        th = routing((NT,), "t")
        not_before = routing((P,), "k", dt=F16, words=P // 2)
        ones16 = routing((P,), "k", dt=F16, words=P // 2)
        n_blk_i = routing((E,), "e", dt=I32)
        n_e, n_blk, blk_end, region, base = [routing((E,), "e") for _ in range(5)]
        assert at[0] <= E * EW // 2

        wat_hi = sb("wat_hi", [P, 4, KD, D], F16)
        wat_lo = sb("wat_lo", [P, 4, KD, D], F16)
        rt_st = sb("rt_st", [P, KD, E])
        rt = sb("rt", [P, KD, 2, E], F16)
        ident32 = sb("ident32", [P, P])
        fill32 = sb("fill32", [P, ROW])
        cols = sb("cols", [P, 4, KD])
        neg_half = sb("neg_half", [P, TPC])
        spare = sb("spare", [P, 7])
        bn = [sb(f"bn{i}", [P, TPC, 6]) for i in range(AHEAD)]
        mv = [sb(f"mv{i}", [P, TPC, 2]) for i in range(AHEAD)]
        stat = [sb(f"stat{i}", [P, 3, TPC]) for i in range(AHEAD)]
        pad_row = sb("pad_row", [1, E], I32)
        blk_e = sb("blk_e", [P, BLOCKS])
        blk_off = sb("blk_off", [1, BLOCKS], I32)
        blk_row = sb("blk_row", [1, BLOCKS], I32)
        pos_i = [sb(f"pos_i{c}", [P, NT], I32) for c in range(TOPK)]

        bankA, bankB, bankC, bankD = [
            ctx.enter_context(nc.psum_tensor(f"bank{n}", [P, 2, 512], F32)) for n in "ABCD"]
        AB = [bankA, bankB]
        logits_ps = bankD[:, 0, 0:NT * E].rearrange("p (t e) -> p t e", t=NT)
        rank_ps = bankD[:, 1, 0:E * NT].rearrange("p (g e t) -> p g e t", g=GROUPS, e=E)
        total_ps = bankD[:, 1, E * NT:2 * E * NT].rearrange("p (g e t) -> p g e t", g=GROUPS, e=E)
        slots_ps = [bankD[:, i, :].rearrange("p (k n) -> p k n", k=KD) for i in range(2)]
        first_slots_ps = bankB[:, 0, :].rearrange("p (k n) -> p k n", k=KD)

        def slots_ps_of(b, i):
            return first_slots_ps if isinstance(b, int) and b == 0 else slots_ps[i]

        x_loaded = [sem(f"x_loaded{i}") for i in range(2)]
        rt_loaded, wat_loaded, cols_loaded, bias_loaded = map(
            sem, ("rt_loaded", "wat_loaded", "cols_loaded", "bias_loaded"))
        wst_loaded = [sem(f"wst_loaded{i}") for i in range(STAGES)]
        consts, pool_step = sem("consts"), sem("pool_step")
        rt_hi, rt_split = sem("rt_hi"), sem("rt_split")
        lam_th, lam_ready, bias_halved = sem("lam_th"), sem("lam_ready"), sem("bias_halved")
        wat_hi_ready, wat_lo_ready = sem("wat_hi_ready"), sem("wat_lo_ready")
        bn_done, x_var, x_rstd, x_norm = map(sem, ("bn_done", "x_var", "x_rstd", "x_norm"))
        xt_ps, xt_hi_ready, xt_lo_ready = map(sem, ("xt_ps", "xt_hi_ready", "xt_lo_ready"))
        logits_done, route_step, chosen_ready, ranks_done = map(
            sem, ("logits_done", "route_step", "chosen_ready", "ranks_done"))
        tops_ready, th_ready, routed = map(sem, ("tops_ready", "th_ready", "routed"))
        blocks_ready, rows_scattered, pads_filled = map(
            sem, ("blocks_ready", "rows_scattered", "pads_filled"))
        v_ps, q_ps, g_ps, yt_ps, zt_ps, o_ps = map(
            sem, ("v_ps", "q_ps", "g_ps", "yt_ps", "zt_ps", "o_ps"))
        states_ready, prod_ready, ybn_done, y_var, y_rstd, z_ready = map(
            sem, ("states_ready", "prod_ready", "ybn_done", "y_var", "y_rstd", "z_ready"))
        w_ready, gate_ready, p_ready, p_hi_ready, p_lo_ready, s_ready = map(
            sem, ("w_ready", "gate_ready", "p_ready", "p_hi_ready", "p_lo_ready", "s_ready"))
        w_hi_ready, w_lo_ready = sem("w_hi_ready"), sem("w_lo_ready")
        x_early_loaded, x_late_loaded = sem("x_early_loaded"), sem("x_late_loaded")
        slot_loaded = [sem(f"slot_loaded{i}") for i in range(2)]
        slot_t_ps, slot_hi_ready, slot_lo_ready, h_ps, y_ps, y_sb = map(
            sem, ("slot_t_ps", "slot_hi_ready", "slot_lo_ready", "h_ps", "y_ps", "y_sb"))
        sil_ready, g_ready, g_hi_ready, g_split = map(
            sem, ("sil_ready", "g_ready", "g_hi_ready", "g_split"))
        meta_ready = sem("meta_ready")
        y_scattered = [sem(f"y_scattered{i}") for i in range(2)]
        y_loaded = [sem(f"y_loaded{c}") for c in range(CH)]
        pool_sum, moe_sum, moe_silu, gated, pool_added, dve_added = map(
            sem, ("pool_sum", "moe_sum", "moe_silu", "gated", "pool_added", "dve_added"))
        stored = sem("stored")

        x_v = x.rearrange("(t p) d -> p t d", p=P)
        out_v = out.rearrange("(t p) d -> p t d", p=P)
        y_v = y_dram.rearrange("(t p c) d -> p t c d", p=P, c=TOPK)
        slots_v = slots_dram.rearrange("(n p) r -> p n r", p=P)
        w_exp_v = w_exp.rearrange("p (n w) -> p n w", w=PIECE)

        block = ctx.enter_context(nc.Block())

        @block.sync
        def _(sp):
            def load_x(g):
                for i in range(2):
                    if not isinstance(g, int) or g >= 2:
                        sp.wait_ge(x_loaded[i], g * 8)
                    sp.dma_start(xst[:, bass.ds(g * TPC + i * TPC, TPC), :],
                                 x_v[:, bass.ds(g * TPC + i * TPC, TPC), :]).then_inc(x_loaded[i], 16)
            repeat(sp, 2, CH, 2, load_x)

            def load_w(c):
                for i in range(PIECES):
                    if not isinstance(c, int) or c * PIECES + i >= STAGES:
                        sp.wait_ge(w_lo_ready, c * PIECES + (i + 1 - STAGES))
                    sp.dma_start(wst[:, i % STAGES, :], w_exp_v[:, bass.ds(c * PIECES + i, 1), :].rearrange(
                        "p a w -> p (a w)")).then_inc(wst_loaded[i % STAGES], 16)
            for c in range(3):
                load_w(c)
            sp.wait_ge(blocks_ready, 1)
            no_tokens = fill32[:, :].unsqueeze(1).to_broadcast([P, SB, ROW])
            sp.dma_start(slots_v[:, E * REGION // P:, :], no_tokens).then_inc(pads_filled, 16)
            for e in range(E):
                row = sp.value_load(pad_row[0:1, e:e + 1], min_val=0, max_val=SLOTS - BLOCK)
                sp.dma_start(slots_dram[bass.ds(row, BLOCK), :].rearrange("(s p) r -> p s r", p=P),
                             no_tokens).then_inc(pads_filled, 16)
            with sp.Fori(3, EARLY) as c:
                load_w(c)

            sp.wait_ge(pads_filled, 16 * (E + 1))
            sp.wait_ge(rows_scattered, 16 * N_SCATTERS)

            def load_slots(b, i):
                if not isinstance(b, int) or b >= 2:
                    sp.wait_ge(slot_t_ps, b - 1)
                    sp.wait_ge(meta_ready, b - 1)
                row = sp.value_load(blk_row[0:1, bass.ds(b, 1)], min_val=0, max_val=E * REGION // P)
                sp.dma_start(slot_in[i], slots_v[:, bass.ds(row, SB), :]).then_inc(slot_loaded[i], 16)

            def two(b):
                load_slots(b, 0)
                load_slots(b + 1, 1)
                for c in range(b - 2, min(b, X_EARLY)) if isinstance(b, int) and b >= 2 else ():
                    if c == 0:
                        sp.wait_ge(w_lo_ready, EARLY * PIECES)
                        sp.wait_ge(p_lo_ready, KD * (EARLY - 1))
                    tiles = slice(c * TPC, (c + 1) * TPC)
                    sp.dma_start(x_early[:, tiles, :], x_v[:, tiles, :]).then_inc(x_early_loaded, 16)
            repeat(sp, X_EARLY + 3, BLOCKS - 1, 2, two)
            load_slots(BLOCKS - 1, (BLOCKS - 1) % 2)

            sp.wait_ge(y_ps, BLOCKS)
            sp.dma_start(x_late, x_v[:, X_EARLY * TPC:, :]).then_inc(x_late_loaded, 16)
            sp.wait_ge(y_scattered[0], 16 * SB * ((BLOCKS + 1) // 2))
            sp.wait_ge(y_scattered[1], 16 * SB * (BLOCKS // 2))

            for c in range(CH):
                sp.dma_start(y_in[c], y_v[:, c * TPC:(c + 1) * TPC, :, :]).then_inc(y_loaded[c], 16)
            for c in range(CH):
                if c < X_POOL:
                    sp.wait_ge(pool_added, c + 1)
                else:
                    sp.wait_ge(dve_added, c + 1 - X_POOL)
                sp.dma_start(out_v[:, c * TPC:(c + 1) * TPC, :], res[c]).then_inc(stored, 16)
            sp.wait_ge(stored, 16 * CH)

        @block.gpsimd
        def _(pool):
            n = [0]

            def step(ins):
                n[0] += 1
                ins.then_inc(pool_step, 1)
                pool.wait_ge(pool_step, n[0])

            step(pool.memset(fill32[:, :], 0.0))
            step(pool.memset(fill32[:, D + META - 1:D + META], NO_ROW))
            pool.nop().then_inc(consts, 1)
            pool.memset(neg_half[:, :], -0.5)
            pool.memset(spare[:, :], 0.0)
            pool.memset(ident32[:, :], 0.0)
            pool.memset(not_before[:, :], -1.0)
            step(pool.memset(ones16[:, :], 1.0))
            pool.affine_select(out=ident32[:, :], in_=ident32[:, :], compare_op=ALU.not_equal, fill=1.0,
                               base=0, pattern=[[-1, P]], channel_multiplier=1)
            step(pool.affine_select(out=not_before[:, :], in_=not_before[:, :], compare_op=ALU.is_ge, fill=0.0,
                                    base=0, pattern=[[-1, P]], channel_multiplier=1))
            pool.nop().then_inc(consts, 1)

            def rstd(i, var_ready, count, out_ready):
                pool.wait_ge(var_ready, count)
                pool.tensor_scalar(stat[i][:, 2, :], mv[i][:, :, 0], -1.0, None, ALU.mult)
                step(pool.tensor_scalar(stat[i][:, 0, :], mv[i][:, :, 1], EPS, None, ALU.add))
                step(pool.tensor_tensor(stat[i][:, 1, :], stat[i][:, 0, :], neg_half[:, :], ALU.pow))
                pool.tensor_tensor(stat[i][:, 2, :], stat[i][:, 2, :], stat[i][:, 1, :],
                                   ALU.mult).then_inc(out_ready, 1)

            for g in range(AHEAD - 1):
                rstd(g, x_var, g + 1, x_rstd)
            pool.iota(e_of[:, :, :], [[0, NT], [1, E]], base=0, channel_multiplier=0,
                      allow_small_or_imprecise_dtypes=True)
            pool.iota(tok_row[:, :], [[2 * P, NT]], base=1, channel_multiplier=2,
                      allow_small_or_imprecise_dtypes=True)
            pool.iota(blk_of[:, :], [[1, BLOCKS]], base=0, channel_multiplier=0,
                      allow_small_or_imprecise_dtypes=True)
            pool.iota(region[:, :], [[REGION, E]], base=0, channel_multiplier=0,
                      allow_small_or_imprecise_dtypes=True)
            step(pool.memset(seg[:, :, :], 1.0))
            step(pool.memset(seg[:, :, 0:1], 0.0))
            pool.nop().then_inc(consts, 1)
            for g in range(AHEAD - 1, CH):
                if g >= AHEAD:
                    pool.wait_ge(x_norm, g + 1 - AHEAD)
                rstd(g % AHEAD, x_var, g + 1, x_rstd)

            scatters = [(pos_i[k][:, t:t + 1], rows[:, t, :]) for t in range(NT) for k in range(TOPK)]

            def scatter(first, end):
                for a in range(first, end):
                    slot, row = scatters[a]
                    if a % (TOPK * GT) == 0:
                        pool.wait_ge(routed, a // (TOPK * GT) + 1)
                    pool.indirect_dma_start(
                        out=slots_dram, out_offset=bass.IndirectOffsetOnAxis(slot, 0),
                        in_=row, in_offset=None,
                        bounds_check=SLOTS - 1, oob_is_err=False).then_inc(rows_scattered, 16)

            done = SCATTERS_FIRST
            scatter(0, done)
            for c in range(EARLY):
                if c >= 1:
                    pool.wait_ge(z_ready, c)
                rstd(0, y_var, c + 1, y_rstd)
                end = min(done + SCATTERS_EACH, N_SCATTERS)
                scatter(done, end)
                done = end

            n_meta = n[0]

            def meta(b, i, first):
                pool.wait_ge(slot_loaded[i], b * 8 + 16 if i == 0 else b * 8 + 8)
                if not first:
                    pool.wait_ge(y_sb, b - 1)
                    pool.wait_ge(y_scattered[i], b * 16 if i == 0 else b * 16 - 16)
                e_b = blk_e[:, bass.ds(b, 1)].to_broadcast([P, SB])
                pool.tensor_tensor(is_first[i][:, :], slot_in[i][:, :, D], e_b, ALU.subtract)\
                    .then_inc(pool_step, 1)
                pool.wait_ge(pool_step, b * 3 + n_meta + 1)
                pool.tensor_tensor(spare[:, i:i + 1], spare[:, 6:7], spare[:, 6:7], ALU.add)
                pool.tensor_scalar(is_first[i][:, :], is_first[i][:, :], 0.0, None, ALU.is_equal)\
                    .then_inc(pool_step, 1)
                pool.wait_ge(pool_step, b * 3 + n_meta + 2)
                pool.tensor_tensor(gate_c[i][:, :], slot_in[i][:, :, D + 1], is_first[i][:, :], ALU.mult)
                pool.tensor_tensor(dest_f[i][:, :], slot_in[i][:, :, D + 3], is_first[i][:, :], ALU.subtract)\
                    .then_inc(pool_step, 1)
                pool.wait_ge(pool_step, b * 3 + n_meta + 3)
                pool.tensor_tensor(gate_c[i][:, :], gate_c[i][:, :], slot_in[i][:, :, D + 2], ALU.add)
                pool.tensor_copy(dest[i][:, :], dest_f[i][:, :]).then_inc(meta_ready, 1)

            def scatter_y(b, i):
                pool.wait_ge(y_sb, b + 1)
                pool.wait_ge(meta_ready, b + 1)
                pool.tensor_tensor(spare[:, 2 + i:3 + i], spare[:, 6:7], spare[:, 6:7], ALU.add)
                for s in range(SB):
                    pool.indirect_dma_start(
                        out=y_dram, out_offset=bass.IndirectOffsetOnAxis(dest[i][:, s:s + 1], 0),
                        in_=ys[i][:, s, :], in_offset=None,
                        bounds_check=ROWS_OUT - 1, oob_is_err=False).then_inc(y_scattered[i], 16)

            pool.wait_ge(rows_scattered, 16 * N_SCATTERS)
            meta(0, 0, True)
            meta(1, 1, True)
            scatter_y(0, 0)
            with pool.Fori(2, BLOCKS - 2, 2) as b:
                meta(b, 0, False)
                scatter_y(b - 1, 1)
                meta(b + 1, 1, False)
                scatter_y(b, 0)
            meta(BLOCKS - 1, 0, False)
            scatter_y(BLOCKS - 2, 1)
            scatter_y(BLOCKS - 1, 0)

            n[0] += 3 * BLOCKS
            pool.wait_ge(x_early_loaded, 16 * X_EARLY)

            def add_x(c):
                pool.wait_ge(gated, c + 1)
                pool.tensor_tensor(res[c], res[c], x_of(c), ALU.add).then_inc(pool_added, 1)

            def sum_y(c):
                pool.wait_ge(y_loaded[c], 16)
                pool.tensor_tensor(res[c], y_in[c][:, :, 0, :], y_in[c][:, :, 1, :], ALU.add)\
                    .then_inc(pool_sum, 1)

            for c in range(EARLY, CH):
                pool.wait_ge(z_ready, c)
                rstd(0, y_var, c + 1, y_rstd)
                if c == EARLY:
                    for early in SUMS_POOL:
                        sum_y(early)
            for c in range(X_POOL):
                add_x(c)

        @block.scalar
        def _(act):
            act.dma_start(rt_st[:, :, :], router).then_inc(rt_loaded, 16)
            for n, a in enumerate((wq, wv, wg, wo)):
                act.dma_start(wat_st[:, n, :, :], a.rearrange("(k p) d -> p k d", p=P))\
                   .then_inc(wat_loaded, 16)
            for n, a in enumerate((beta, ln_g, ln_b)):
                act.dma_start(cols[:, n, :], a).then_inc(cols_loaded, 16)
            act.wait_ge(consts, 2)
            act.activation(spare[:, 3:4], spare[:, 2:3], ACT.Silu)
            act.wait_ge(rt_loaded, 16)
            act.activation(rt[:, :, 0, :], rt_st[:, :, :], ACT.Copy, scale=WSCALE).then_inc(rt_hi, 1)

            def norm_x(g):
                i = g % AHEAD
                act.wait_ge(x_rstd, g + 1)
                for j in range(g * TPC, (g + 1) * TPC):
                    last = act.activation(rows[:, j, 0:D], xst[:, j, :], ACT.Identity,
                                          bias=stat[i][:, 2, j % TPC:j % TPC + 1],
                                          scale=stat[i][:, 1, j % TPC:j % TPC + 1])
                last.then_inc(x_norm, 1)

            def high_xt(g, i):
                act.wait_ge(xt_ps, g + 1)
                act.activation(xnT[:, g, 0:KD, :], AB[i][:, :, :], ACT.Copy).then_inc(xt_hi_ready, 1)

            def route_gates(g):
                tiles = slice(g * GT, (g + 1) * GT)
                act.wait_ge(tops_ready, g + 1)
                act.activation(th[:, tiles], th[:, tiles], ACT.Tanh, scale=0.5 / WSCALE).then_inc(th_ready, 1)

            norm_x(0)
            act.wait_ge(cols_loaded, 48)
            act.activation(cols[:, 3, :], cols[:, 0, :], ACT.Tanh, scale=0.5).then_inc(lam_th, 1)
            for g in range(1, CH):
                norm_x(g)
                high_xt(g - 1, 1 - g % 2)
                if g == GC + 1:
                    act.wait_ge(wat_loaded, 64)
                    act.activation(wat_hi[:, :, :, :], wat_st, ACT.Copy, scale=WSCALE)\
                       .then_inc(wat_hi_ready, 1)
                if g == GC + 2:
                    route_gates(0)
            high_xt(CH - 1, 1)
            route_gates(1)

            def affine(c, buffers=early_buffers):
                _, w, _, _ = buffers
                act.wait_ge(zt_ps, c)
                if not isinstance(c, int) or c >= 2:
                    act.wait_ge(p_lo_ready, KD * (c - 1))
                for m in range(KD):
                    act.activation(w[:, m, :], bankD[:, m, :], ACT.Identity, bias=cols[:, 2, m:m + 1],
                                   scale=cols[:, 1, m:m + 1]).then_inc(w_ready, 1)

            def split_p(c, buffers=early_buffers):
                _, w, p_hi, _ = buffers
                if not isinstance(c, int) or c >= 2:
                    act.wait_ge(o_ps, c - 1)
                for m in range(KD):
                    act.wait_ge(p_ready, KD * (c - 1) + m + 1)
                    act.activation(p_hi[:, m, :], w[:, m, :], ACT.Copy).then_inc(p_hi_ready, 1)

            def convert_w(c, i):
                act.wait_ge(wst_loaded[i % STAGES], c * (PIECES // STAGES * 16) + (i // STAGES * 16 + 16))
                act.activation(w_hi[:, bass.ds((c * PIECES + i) * PIECE, PIECE)], wst[:, i % STAGES, :],
                               ACT.Copy, scale=WSCALE).then_inc(w_hi_ready, 1)

            def keep_s(c):
                act.wait_ge(o_ps, c)
                act.activation(s_all[:, bass.ds(c * TPC - TPC, TPC), :].rearrange("p t d -> p (t d)"),
                               bankC[:, :, :].rearrange("p a b -> p (a b)"), ACT.Copy,
                               scale=1.0 / WSCALE).then_inc(s_ready, 1)

            def silu_moe(*chunks):
                for c in chunks:
                    if c in SUMS_POOL:
                        act.wait_ge(pool_sum, SUMS_POOL.index(c) + 1)
                    else:
                        act.wait_ge(moe_sum, c + 1 - sum(p < c for p in SUMS_POOL))
                    act.activation(res[c], res[c], ACT.Silu).then_inc(moe_silu, 1)

            def recur(c, convert=True, between=(), buffers=early_buffers, last_early=False):
                later = not isinstance(c, int) or c >= 1
                if later:
                    affine(c, buffers)
                    split_p(c, buffers)
                act.wait_ge(g_ps, c + 1)
                if later:
                    act.wait_ge(p_ready, KD * c)
                act.activation(gate, bankC[:, :, :], ACT.Silu, scale=1.0 / WSCALE).then_inc(gate_ready, 1)
                for i in range(PIECES if convert else 0):
                    convert_w(c, i)
                silu_moe(*between)
                if last_early:
                    act.wait_ge(rows_scattered, 16 * N_SCATTERS)
                    high_slots(0, 0, True)
                act.wait_ge(y_rstd, c + 1)
                if later:
                    act.wait_ge(zt_ps, c)
                for j in range(TPC):
                    last = act.activation(z[:, j, :], bankD[:, j // 2, j % 2 * D:j % 2 * D + D],
                                          ACT.Identity, bias=stat[0][:, 2, j:j + 1],
                                          scale=stat[0][:, 1, j:j + 1])
                last.then_inc(z_ready, 1)
                if later:
                    keep_s(c)

            def high_slots(b, i, first):
                act.wait_ge(slot_t_ps, b + 1)
                if not first:
                    act.wait_ge(h_ps, b * 2 - 2)
                act.activation(xT[i][:, 0:KD, :], slots_ps_of(b, i), ACT.Copy).then_inc(slot_hi_ready, 1)

            def halves(b, i, before, last=False):
                for j in range(2):
                    if j == 1 and not last:
                        high_slots(b + 1, 1 - i, before == 0)
                    act.wait_ge(h_ps, b * 2 + j + 1)
                    if before >= 1:
                        act.wait_ge(g_ready, b * 2 - 1 + j)
                    act.activation(sil[j], AB[j][:, :, 0:BLOCK], ACT.Silu,
                                   scale=1.0 / WSCALE).then_inc(sil_ready, 1)
                    act.wait_ge(g_ready, b * 2 + j + 1)
                    if before >= 2:
                        act.wait_ge(y_ps, b - 1)
                    act.activation(g_hi[i][:, 2 * j:2 * j + 2, :], g32[j], ACT.Copy)\
                       .then_inc(g_hi_ready, 1)

            repeat(act, 1, EARLY - 1, 1, recur)
            recur(EARLY - 1, last_early=True)
            act.dma_start(half_bias, bias).then_inc(bias_loaded, 16)
            halves(0, 0, 0)
            act.wait_ge(bias_loaded, 16)
            act.activation(half_bias, half_bias, ACT.Copy, scale=0.5).then_inc(bias_halved, 1)
            halves(1, 1, 1)
            with act.Fori(2, BLOCKS - 2, 2) as b:
                halves(b, 0, 2)
                halves(b + 1, 1, 2)
            halves(BLOCKS - 1, 0, 2, last=True)

            recur(EARLY, False, (0,), late_buffers)
            recur(CH - 1, False, SUMS_POOL, late_buffers)
            affine(CH, late_buffers)
            split_p(CH, late_buffers)
            silu_moe(*range(len(SUMS_POOL) + 1, CH))

        @block.vector
        def _(dve):
            n = [0]

            def step(ins):
                n[0] += 1
                ins.then_inc(route_step, 1)
                dve.wait_ge(route_step, n[0])

            def stats_x(g):
                i = g % AHEAD
                dve.wait_ge(x_loaded[g % 2], g // 2 * 16 + 16)
                if g >= AHEAD:
                    dve.wait_ge(x_var, g + 1 - AHEAD)
                for j in range(TPC):
                    last = dve.bn_stats(bn[i][:, j, :], xst[:, g * TPC + j, :])
                last.then_inc(bn_done, 1)
                dve.wait_ge(bn_done, g + 1)
                if g >= AHEAD:
                    dve.wait_ge(x_rstd, g + 1 - AHEAD)
                for j in range(TPC):
                    last = dve.bn_aggr(mv[i][:, j, :], bn[i][:, j, :])
                last.then_inc(x_var, 1)

            def low_xt(g, i):
                dve.wait_ge(xt_hi_ready, g + 1)
                dve.tensor_tensor(xnT[:, g, KD:2 * KD, :], AB[i][:, :, :], xnT[:, g, 0:KD, :],
                                  ALU.subtract).then_inc(xt_lo_ready, 1)

            dve.wait_ge(consts, 2)
            stats_x(0)
            dve.wait_ge(rt_hi, 1)
            dve.scalar_tensor_tensor(rt[:, :, 1, :], rt_st[:, :, :], WSCALE, rt[:, :, 0, :],
                                     ALU.mult, ALU.subtract).then_inc(rt_split, 1)
            for g in range(1, AHEAD - 1):
                stats_x(g)
            dve.wait_ge(lam_th, 1)
            dve.tensor_scalar(cols[:, 3, :], cols[:, 3, :], 0.5, 0.5, ALU.mult, ALU.add)\
               .then_inc(lam_ready, 1)
            def choose(g):
                tiles = slice(g * GT, (g + 1) * GT)

                def by_token(a):
                    return a[:, tiles].unsqueeze(2).to_broadcast([P, GT, E])

                lg_g, lg2_g = logits_ps[:, tiles, :], lg2[:, tiles, :]
                cand_g, e_g = cand[:, tiles, :], e_of[:, tiles, :]
                dve.wait_ge(logits_done, (g + 1) * GC)
                dve.wait_ge(consts, 3)
                for c, src in enumerate((lg_g, lg2_g)):
                    step(dve.tensor_reduce(top[c][:, tiles], src, AX.X, ALU.max))
                    step(dve.tensor_tensor(cand_g, src, by_token(top[c]), ALU.is_equal))
                    step(dve.scalar_tensor_tensor(cand_g, cand_g, -16.0, e_g, ALU.mult, ALU.add))
                    step(dve.tensor_reduce(least[c][:, tiles], cand_g, AX.X, ALU.min))
                    step(dve.tensor_tensor(oh[c][:, tiles, :], cand_g, by_token(least[c]), ALU.is_equal))
                    if c == 0:
                        step(dve.scalar_tensor_tensor(lg2_g, oh[0][:, tiles, :], MASKED, lg_g,
                                                      ALU.mult, ALU.add))
                dve.tensor_tensor(chosen[:, g, :, :].rearrange("p e t -> p t e"), oh[0][:, tiles, :],
                                  oh[1][:, tiles, :], ALU.add).then_inc(chosen_ready, 1)
                dve.tensor_tensor(th[:, tiles], top[0][:, tiles], top[1][:, tiles], ALU.subtract)\
                   .then_inc(tops_ready, 1)

            def count(g):
                run_g, slot_g = run[:, g, :, :], slot_of[:, g, :, :]
                flat = "p e t -> p (e t)"
                dve.wait_ge(ranks_done, g + 1)
                step(dve.tensor_tensor_scan(run_g.rearrange(flat), seg[:, :, :].rearrange(flat),
                                            total_ps[:, g, :, :].rearrange(flat), 0.0, ALU.mult, ALU.add))
                step(dve.tensor_tensor(slot_g, run_g, rank_ps[:, g, :, :], ALU.add))

            def place(g):
                tiles = slice(g * GT, (g + 1) * GT)
                slot_g, cand_g = slot_of[:, g, :, :], cand[:, tiles, :]
                start = region if g == 0 else base
                step(dve.tensor_tensor(slot_g, slot_g, start[:, :].unsqueeze(2).to_broadcast([P, E, GT]),
                                       ALU.add))
                for c in range(TOPK):
                    step(dve.tensor_tensor(cand_g, oh[c][:, tiles, :], slot_g.rearrange("p e t -> p t e"),
                                           ALU.mult))
                    step(dve.tensor_reduce(pos[c][:, tiles], cand_g, AX.X, ALU.add))
                    dve.tensor_copy(pos_i[c][:, tiles], pos[c][:, tiles])
                dve.tensor_copy(rows[:, tiles, D], least[0][:, tiles])
                dve.tensor_copy(rows[:, tiles, D + 3], tok_row[:, tiles])
                dve.wait_ge(th_ready, g + 1)
                dve.tensor_scalar(rows[:, tiles, D + 1], th[:, tiles], 1.0 / WSCALE, None, ALU.mult)
                dve.tensor_scalar(rows[:, tiles, D + 2], th[:, tiles], -0.5 / WSCALE, 0.5 / WSCALE,
                                  ALU.mult, ALU.add).then_inc(routed, 1)
                if g == 0:
                    step(dve.tensor_tensor(base[:, :], region[:, :], run[:, 0, :, GT - 1], ALU.add))

            for g in range(CH):
                if g + AHEAD - 1 < CH:
                    stats_x(g + AHEAD - 1)
                low_xt(g, g % 2)
                if g == GC:
                    choose(0)
                    dve.wait_ge(wat_hi_ready, 1)
                    dve.scalar_tensor_tensor(wat_lo[:, :, :, :], wat_st, WSCALE, wat_hi[:, :, :, :],
                                             ALU.mult, ALU.subtract).then_inc(wat_lo_ready, 1)
                if g == GC + 1:
                    count(0)
                    place(0)
            choose(1)

            def count_blocks():
                step(dve.tensor_tensor(n_e[:, :], run[:, 0, :, GT - 1], run[:, 1, :, GT - 1], ALU.add))
                step(dve.tensor_scalar(n_blk_i[:, :], n_e[:, :], float(BLOCK - 1), None, ALU.add))
                step(dve.tensor_single_scalar(n_blk_i[:, :], n_blk_i[:, :], BLOCK.bit_length() - 1,
                                              ALU.logical_shift_right))
                step(dve.tensor_copy(n_blk[:, :], n_blk_i[:, :]))
                step(dve.tensor_tensor_scan(blk_end[:, :], seg[:, 0, 1:E + 1], n_blk[:, :], 0.0,
                                            ALU.mult, ALU.add))

            def list_blocks():
                by_block = [P, BLOCKS, E]
                step(dve.tensor_tensor(blk_le[:, :, :], blk_end[:, :].unsqueeze(1).to_broadcast(by_block),
                                       blk_of[:, :].unsqueeze(2).to_broadcast(by_block), ALU.is_le))
                dve.tensor_tensor(blk_n[:, :, :], blk_le[:, :, :],
                                  n_blk[:, :].unsqueeze(1).to_broadcast(by_block), ALU.mult)
                step(dve.tensor_reduce(blk_e8[:, :], blk_le[:, :, :], AX.X, ALU.add))
                step(dve.tensor_reduce(blk_s[:, :], blk_n[:, :, :], AX.X, ALU.add))
                step(dve.tensor_tensor(blk_row_f[:, :], blk_of[:, :], blk_s[:, :], ALU.subtract))
                step(dve.scalar_tensor_tensor(blk_row_f[:, :], blk_e8[:, :], float(REGION // BLOCK),
                                              blk_row_f[:, :], ALU.mult, ALU.add))
                dve.tensor_scalar(blk_row[:, :], blk_row_f[0:1, :], float(SB), float(E * REGION // P),
                                  ALU.mult, ALU.min)
                step(dve.tensor_single_scalar(blk_e8[:, :], blk_e8[:, :], float(E - 1), ALU.min))
                dve.tensor_single_scalar(blk_off[:, :], blk_e8[0:1, :], float(EW), ALU.mult)
                dve.tensor_single_scalar(blk_e[:, :], blk_e8[:, :], -16.0, ALU.add)
                dve.tensor_tensor(pad_row[:, :], region[0:1, :], n_e[0:1, :], ALU.add)\
                   .then_inc(blocks_ready, 1)

            dve.wait_ge(lam_ready, 1)

            def recur(c, convert=True, buffers=early_buffers):
                states, _, _, _ = buffers
                later = not isinstance(c, int) or c >= 1
                dve.wait_ge(v_ps, c + 1)
                if later:
                    dve.wait_ge(yt_ps, c)
                for m in range(KD):
                    last = dve.tensor_tensor_scan(states[:, m, :], cols[:, 3, m:m + 1].to_broadcast([P, S]),
                                                  bankA[:, m, :], 0.0, ALU.mult, ALU.add)
                last.then_inc(states_ready, 1)
                if not later:
                    count(1)
                    count_blocks()
                dve.wait_ge(q_ps, c + 1)
                dve.wait_ge(states_ready, c + 1)
                dve.scalar_tensor_tensor(states, bankB[:, :, :], 1.0 / WSCALE ** 2, states,
                                         ALU.mult, ALU.mult).then_inc(prod_ready, 1)
                if later:
                    times_gate(c, buffers)
                else:
                    place(1)
                dve.wait_ge(yt_ps, c + 1)
                if later:
                    dve.wait_ge(y_var, c)
                else:
                    dve.wait_ge(x_var, CH)
                for j in range(TPC):
                    last = dve.bn_stats(bn[0][:, j, :], bankD[:, j // 2, j % 2 * D:j % 2 * D + D])
                last.then_inc(ybn_done, 1)
                dve.wait_ge(ybn_done, c + 1)
                if later:
                    dve.wait_ge(y_rstd, c)
                dve.memset(spare[:, 4:5], 0.0)
                for j in range(TPC):
                    last = dve.bn_aggr(mv[0][:, j, :], bn[0][:, j, :])
                last.then_inc(y_var, 1)
                if isinstance(c, int) and c == 1:
                    list_blocks()
                for i in range(PIECES if convert else 0):
                    dve.wait_ge(w_hi_ready, c * PIECES + (i + 1))
                    piece = bass.ds((c * PIECES + i) * PIECE, PIECE)
                    dve.scalar_tensor_tensor(w_lo[:, piece], wst[:, i % STAGES, :], WSCALE, w_hi[:, piece],
                                             ALU.mult, ALU.subtract).then_inc(w_lo_ready, 1)

            def times_gate(c, buffers):
                _, w, p_hi, p_lo = buffers
                for m in range(KD):
                    dve.wait_ge(w_ready, KD * (c - 1) + m + 1)
                    if m == 0:
                        dve.wait_ge(gate_ready, c)
                    dve.tensor_tensor(w[:, m, :], w[:, m, :], gate[:, m, :], ALU.mult).then_inc(p_ready, 1)
                for m in range(KD):
                    dve.wait_ge(p_hi_ready, KD * (c - 1) + m + 1)
                    dve.tensor_tensor(p_lo[:, m, :], w[:, m, :], p_hi[:, m, :], ALU.subtract)\
                       .then_inc(p_lo_ready, 1)

            repeat(dve, 2, EARLY, 1, recur)

            dve.wait_ge(rows_scattered, 16 * N_SCATTERS)

            def low_slots(b, i):
                dve.wait_ge(slot_hi_ready, b + 1)
                dve.tensor_tensor(xT[i][:, KD:2 * KD, :], slots_ps_of(b, i), xT[i][:, 0:KD, :],
                                  ALU.subtract).then_inc(slot_lo_ready, 1)

            def half(b, i, j):
                dve.wait_ge(sil_ready, b * 2 + j + 1)
                dve.scalar_tensor_tensor(g32[j], sil[j], 1.0 / WSCALE, AB[j][:, :, BLOCK:2 * BLOCK],
                                         ALU.mult, ALU.mult).then_inc(g_ready, 1)
                dve.wait_ge(g_hi_ready, b * 2 + j + 1)
                dve.tensor_tensor(g_lo[i][:, 2 * j:2 * j + 2, :], g32[j], g_hi[i][:, 2 * j:2 * j + 2, :],
                                  ALU.subtract).then_inc(g_split, 1)

            def gate_y(b, i, first):
                dve.wait_ge(y_ps, b + 1)
                dve.wait_ge(meta_ready, b + 1)
                if not first:
                    dve.wait_ge(y_scattered[i], b * 16 if i == 0 else b * 16 - 16)
                for s in range(SB):
                    last = dve.scalar_tensor_tensor(ys[i][:, s, :], bankC[:, i, s * D:s * D + D],
                                                    gate_c[i][:, s:s + 1], half_bias,
                                                    ALU.mult, ALU.add)
                last.then_inc(y_sb, 1)

            def halves(b, i, last=False):
                half(b, i, 0)
                if not last:
                    low_slots(b + 1, 1 - i)
                half(b, i, 1)

            low_slots(0, 0)
            halves(0, 0)
            halves(1, 1)
            dve.wait_ge(bias_halved, 1)
            gate_y(0, 0, True)
            with dve.Fori(2, BLOCKS - 2, 2) as b:
                halves(b, 0)
                gate_y(b - 1, 1, False)
                halves(b + 1, 1)
                gate_y(b, 0, False)
            halves(BLOCKS - 1, 0, True)
            gate_y(BLOCKS - 2, 1, False)
            gate_y(BLOCKS - 1, 0, False)

            def sum_y(c):
                dve.wait_ge(y_loaded[c], 16)
                dve.tensor_tensor(res[c], y_in[c][:, :, 0, :], y_in[c][:, :, 1, :], ALU.add)\
                   .then_inc(moe_sum, 1)

            def finish(c):
                dve.wait_ge(moe_silu, c + 1)
                if c < CH - 1:
                    dve.wait_ge(s_ready, c + 1)
                    dve.tensor_tensor(res[c], res[c], s_all[:, c * TPC:(c + 1) * TPC, :], ALU.mult)\
                       .then_inc(gated, 1)
                else:
                    dve.wait_ge(o_ps, CH)
                    s_ps = bankC[:, :, :].rearrange("p a (t d) -> p (a t) d", d=D)
                    dve.scalar_tensor_tensor(res[c], s_ps, 1.0 / WSCALE, res[c], ALU.mult, ALU.mult)\
                       .then_inc(gated, 1)

            def add_x(c):
                dve.wait_ge(gated, c + 1)
                dve.wait_ge(x_early_loaded, 16 * X_EARLY)
                dve.wait_ge(x_late_loaded, 16)
                dve.tensor_tensor(res[c], res[c], x_of(c), ALU.add).then_inc(dve_added, 1)

            recur(EARLY, False, late_buffers)
            sum_y(0)
            finish(0)
            recur(CH - 1, False, late_buffers)
            for c in range(1, 4):
                finish(c)
            sum_y(5)
            sum_y(6)
            times_gate(CH, late_buffers)
            finish(4)
            sum_y(7)
            for c in range(5, CH):
                finish(c)
            for c in range(X_POOL, CH):
                add_x(c)

        @block.tensor
        def _(pe):
            def three(out_ap, pairs, hi_l, lo_l, hi_r, lo_r):
                todo = [(a(k), b(k)) for k in pairs for a, b in ((hi_l, hi_r), (hi_l, lo_r), (lo_l, hi_r))]
                for n, (lhsT, rhs) in enumerate(todo):
                    last = pe.matmul(out_ap, lhsT, rhs, start=(n == 0), stop=(n == len(todo) - 1))
                return last

            pe.wait_ge(consts, 2)

            def transpose_x(g, i):
                pe.wait_ge(x_norm, g + 1)
                if g >= 2:
                    pe.wait_ge(xt_lo_ready, g - 1)
                for j in range(TPC):
                    for k in range(KD):
                        last = pe.transpose(AB[i][:, k, j * P:j * P + P],
                                            rows[:, g * TPC + j, k * P:k * P + P], ident32[:, :])
                last.then_inc(xt_ps, 1)

            def route_x(g):
                pe.wait_ge(xt_lo_ready, g + 1)
                for j in range(TPC):
                    for q in range(2 * KD):
                        for h in range(2):
                            last = pe.matmul(logits_ps[:, g * TPC + j, :], xnT[:, g, q, j * P:j * P + P],
                                             rt[:, q % KD, h, :], start=(q == 0 and h == 0),
                                             stop=(q == 2 * KD - 1 and h == 1))
                return last

            def count_ranks(g):
                pe.wait_ge(chosen_ready, g + 1)
                chosen_g = chosen[:, g, :, :].rearrange("p e t -> p (e t)")
                pe.matmul(rank_ps[:, g, :, :].rearrange("p e t -> p (e t)"), not_before[:, :], chosen_g,
                          start=True, stop=True)
                pe.matmul(total_ps[:, g, :, :].rearrange("p e t -> p (e t)"), ones16[:, :], chosen_g,
                          start=True, stop=True).then_inc(ranks_done, 1)

            def project_half(bank, a, c, m):
                return three(bank[:, m, :], range(KD),
                             lambda k: wat_hi[:, a, k, m * P:m * P + P],
                             lambda k: wat_lo[:, a, k, m * P:m * P + P],
                             lambda k: xnT[:, bass.ds(c, 1), k, :].rearrange("p a n -> p (a n)"),
                             lambda k: xnT[:, bass.ds(c, 1), KD + k, :].rearrange("p a n -> p (a n)"))

            def project(bank, a, c):
                project_half(bank, a, c, 0)
                return project_half(bank, a, c, 1)

            transpose_x(0, 0)
            pe.wait_ge(rt_split, 1)
            for g in range(1, CH - 1):
                transpose_x(g, g % 2)
                if g == GC + 1:
                    count_ranks(0)
                if g < CH - 2:
                    route_x(g - 1).then_inc(logits_done, 1)
            pe.wait_ge(wat_lo_ready, 1)
            project_half(bankC, 2, 0, 0)
            transpose_x(CH - 1, 1)
            project_half(bankC, 2, 0, 1).then_inc(g_ps, 1)
            for g in range(CH - 3, CH):
                route_x(g).then_inc(logits_done, 1)

            def transpose_z(c, after_blocks=False):
                pe.wait_ge(z_ready, c)
                if after_blocks:
                    pe.wait_ge(slot_lo_ready, BLOCKS)
                for j in range(TPC):
                    for m in range(KD):
                        last = pe.transpose(bankD[:, m, j * P:j * P + P], z[:, j, m * P:m * P + P],
                                            ident32[:, :])
                last.then_inc(zt_ps, 1)

            def project_out(c, buffers):
                _, _, p_hi, p_lo = buffers
                pe.wait_ge(p_lo_ready, KD * c)
                for j in range(TPC):
                    last = three(bankC[:, j // 2, j % 2 * D:j % 2 * D + D], range(KD),
                                 lambda k: p_hi[:, k, j * P:j * P + P],
                                 lambda k: p_lo[:, k, j * P:j * P + P],
                                 lambda k: wat_hi[:, 3, k, :],
                                 lambda k: wat_lo[:, 3, k, :])
                last.then_inc(o_ps, 1)

            def recur(c, after_blocks=False, buffers=early_buffers, last=False):
                states, _, _, _ = buffers
                later = not isinstance(c, int) or c >= 1
                if later:
                    pe.wait_ge(prod_ready, c)
                project(bankB, 0, c).then_inc(q_ps, 1)
                if later:
                    transpose_z(c, after_blocks)
                if not isinstance(c, int) or c >= 2:
                    pe.wait_ge(s_ready, c - 1)
                if later:
                    project(bankC, 2, c).then_inc(g_ps, 1)
                pe.wait_ge(prod_ready, c + 1)
                if later:
                    pe.wait_ge(w_ready, KD * c)
                for j in range(TPC):
                    for m in range(KD):
                        y_t = pe.transpose(bankD[:, j // 2, j % 2 * D + m * P:j % 2 * D + m * P + P],
                                            states[:, m, j * P:j * P + P], ident32[:, :])
                y_t.then_inc(yt_ps, 1)
                if not last:
                    pe.wait_ge(states_ready, c + 1)
                    project(bankA, 1, c + 1).then_inc(v_ps, 1)
                if later:
                    pe.wait_ge(gate_ready, c + 1)
                    project_out(c, buffers)

            project(bankA, 1, 0).then_inc(v_ps, 1)
            count_ranks(1)
            repeat(pe, 1, EARLY - 1, 1, recur)
            recur(EARLY - 1, last=True)

            def weights_at(b):
                return pe.value_load(blk_off[0:1, bass.ds(b, 1)], min_val=0, max_val=(E - 1) * EW)

            def transpose_slots(b, i, first):
                pe.wait_ge(slot_loaded[i], b * 8 + 16 if i == 0 else b * 8 + 8)
                if not first:
                    pe.wait_ge(slot_lo_ready, b - 1)
                for k in range(KD):
                    for s in range(SB):
                        last = pe.transpose(slots_ps_of(b, i)[:, k, s * P:s * P + P],
                                            slot_in[i][:, s, k * P:k * P + P], ident32[:, :])
                last.then_inc(slot_t_ps, 1)

            def hidden(b, i, j, off, first):
                if not first:
                    pe.wait_ge(g_ready, b * 2 - 1 + j)
                for m in (2 * j, 2 * j + 1):
                    for half in range(2):
                        col = half * HID + m * P
                        last = three(AB[j][:, m % 2, half * BLOCK:half * BLOCK + BLOCK], range(KD),
                                     lambda k: w_hi[:, bass.ds(off + (k * 2 * HID + col), P)],
                                     lambda k: w_lo[:, bass.ds(off + (k * 2 * HID + col), P)],
                                     lambda k: xT[i][:, k, :],
                                     lambda k: xT[i][:, KD + k, :])
                last.then_inc(h_ps, 1)

            def outputs(b, i, off, first):
                pe.wait_ge(g_split, b * 2 + 2)
                if first:
                    pe.wait_ge(s_ready, EARLY - 1)
                else:
                    pe.wait_ge(y_sb, b - 1)
                for s in range(SB):
                    last = three(bankC[:, i, s * D:s * D + D], range(KH),
                                 lambda k: g_hi[i][:, k, s * P:s * P + P],
                                 lambda k: g_lo[i][:, k, s * P:s * P + P],
                                 lambda k: w_hi[:, bass.ds(off + (KD * 2 * HID + k * D), D)],
                                 lambda k: w_lo[:, bass.ds(off + (KD * 2 * HID + k * D), D)])
                last.then_inc(y_ps, 1)

            def one_block(b, i, first=False, last=False, second=False):
                off = weights_at(b)
                pe.wait_ge(slot_lo_ready, b + 1)
                hidden(b, i, 0, off, first)
                if first:
                    pe.wait_ge(z_ready, EARLY)
                if not last:
                    transpose_slots(b + 1, 1 - i, first)
                hidden(b, i, 1, off, first)
                if not first:
                    outputs(b - 1, 1 - i, weights_at(b - 1), second)

            transpose_slots(0, 0, True)
            pe.wait_ge(w_lo_ready, EARLY * PIECES)
            one_block(0, 0, first=True)
            one_block(1, 1, second=True)
            with pe.Fori(2, BLOCKS - 2, 2) as b:
                one_block(b, 0)
                one_block(b + 1, 1)
            one_block(BLOCKS - 1, 0, last=True)
            outputs(BLOCKS - 1, 0, weights_at(BLOCKS - 1), False)

            pe.wait_ge(g_ready, 2 * BLOCKS)
            pe.wait_ge(y_sb, BLOCKS)
            project(bankA, 1, EARLY).then_inc(v_ps, 1)
            for c in range(EARLY, CH):
                recur(c, c == EARLY, late_buffers, c == CH - 1)
            transpose_z(CH)
            project_out(CH, late_buffers)


_OUT_SHAPE = (B, S, D)


def kernel(L0_attn_x, L0_attn_Wq, L0_attn_Wv, L0_attn_Wg, L0_attn_Wo, L0_attn_beta, L0_attn_ln_g,
           L0_attn_ln_b, L0_ffn_router_weight, L0_ffn_w_in, L0_ffn_w_out, L0_ffn_bias):
    import concourse.bacc as bacc
    from concourse.bass_utils import run_bass_kernel_spmd

    def by_partition(a):
        return np.ascontiguousarray(a.reshape(KD, P, -1).transpose(1, 0, 2))

    def column(a):
        return np.ascontiguousarray(a.reshape(KD, P).T)

    w_in = np.asarray(L0_ffn_w_in).reshape(E, 2 * HID, KD, P).transpose(3, 0, 2, 1)
    w_out = np.asarray(L0_ffn_w_out).reshape(E, D, KH, P).transpose(3, 0, 2, 1)
    w_exp = np.concatenate([w_in.reshape(P, E, -1), w_out.reshape(P, E, -1)], axis=2).reshape(P, E * EW)
    arrays = {
        "x": np.asarray(L0_attn_x).reshape(T, D),
        "wq": np.asarray(L0_attn_Wq), "wv": np.asarray(L0_attn_Wv),
        "wg": np.asarray(L0_attn_Wg), "wo": np.asarray(L0_attn_Wo),
        "beta": column(np.repeat(np.asarray(L0_attn_beta), D // NH)),
        "ln_g": column(np.asarray(L0_attn_ln_g)), "ln_b": column(np.asarray(L0_attn_ln_b)),
        "router": by_partition(np.asarray(L0_ffn_router_weight).T),
        "w_exp": w_exp,
        "bias": np.broadcast_to(np.asarray(L0_ffn_bias), (P, D)),
    }
    arrays = {f"{k}_in": np.ascontiguousarray(v) for k, v in arrays.items()}
    nc = bacc.Bacc("TRN2", target_bir_lowering=False, num_devices=1)
    args = [nc.dram_tensor(k, v.shape, mybir.dt.from_np(v.dtype), kind="ExternalInput").ap()
            for k, v in arrays.items()]
    out = nc.dram_tensor("out", (T, D), F32, kind="ExternalOutput").ap()
    build(nc, *args, out)
    r = run_bass_kernel_spmd(nc, [arrays], core_ids=[0])
    return r.results[0]["out"].reshape(_OUT_SHAPE)
```
